# Optimizing a Trainium2 kernel written in Bass

```python
import numpy as np
import jax
import jax.numpy as jnp

def _softmax(x, axis=-1):
    return jax.nn.softmax(x, axis=axis)

def _gelu(x):
    return jax.nn.gelu(x, approximate=True)

def _silu(x):
    return jax.nn.silu(x)

def _sigmoid(x):
    return jax.nn.sigmoid(x)

def _layernorm(x, axis=-1, eps=1e-05):
    m = jnp.mean(x, axis=axis, keepdims=True)
    v = jnp.var(x, axis=axis, keepdims=True)
    return (x - m) / jnp.sqrt(v + eps)

def _scatter_add(tgt, idx, src, axis=0):
    return tgt.at[idx].add(src)

def _segment_sum(src, seg, n):
    return jax.ops.segment_sum(src, seg, n)
kernel_name = 'mk_seq_postln_d1_jaxref_r8_26844a'

def setup_inputs(seed: int=0):
    np.random.seed(seed)
    _w = jnp.asarray

    def _L0_attn_setup():
        import jax, jax.numpy as jnp
        import numpy as np
        B, T, C, H = (2, 128, 128, 16)
        D = C // H
        EPS = 1e-06
        key = jax.random.key(seed)
        k1, k2, k3, k4, k5 = jax.random.split(key, 5)
        s = 0.02
        return {'x': jax.random.normal(k1, (B, T, C), dtype=jnp.float32), 'w_qkv': jax.random.normal(k2, (3 * C, C), dtype=jnp.float32) * s, 'b_qkv': jax.random.normal(k3, (3 * C,), dtype=jnp.float32) * s, 'w_out': jax.random.normal(k4, (C, C), dtype=jnp.float32) * s, 'b_out': jax.random.normal(k5, (C,), dtype=jnp.float32) * s}
    _L0_attn_in = _L0_attn_setup()

    def _L0_ffn_setup():
        import jax, jax.numpy as jnp
        import numpy as np
        TOP_K = 2
        key = jax.random.key(seed)
        k1, k2, k3, k4, k5 = jax.random.split(key, 5)
        B, S, D, F, E = (2, 128, 128, 256, 8)
        return {'x': jax.random.normal(k1, (B, S, D), dtype=jnp.float32), 'router_kernel_DE': jax.random.normal(k2, (D, E), dtype=jnp.float32) * 0.02, 'kernel_gating_EDF': jax.random.normal(k3, (E, D, F), dtype=jnp.float32) * 0.02, 'kernel_up_EDF': jax.random.normal(k4, (E, D, F), dtype=jnp.float32) * 0.02, 'kernel_down_EFD': jax.random.normal(k5, (E, F, D), dtype=jnp.float32) * 0.02}
    _L0_ffn_in = _L0_ffn_setup()
    _d = {'L0_attn_x': _L0_attn_in['x'], 'L0_attn_w_qkv': _L0_attn_in['w_qkv'], 'L0_attn_b_qkv': _L0_attn_in['b_qkv'], 'L0_attn_w_out': _L0_attn_in['w_out'], 'L0_attn_b_out': _L0_attn_in['b_out'], 'L0_ffn_router_kernel_DE': _L0_ffn_in['router_kernel_DE'], 'L0_ffn_kernel_gating_EDF': _L0_ffn_in['kernel_gating_EDF'], 'L0_ffn_kernel_up_EDF': _L0_ffn_in['kernel_up_EDF'], 'L0_ffn_kernel_down_EFD': _L0_ffn_in['kernel_down_EFD']}
    _x0 = _d['L0_attn_x']
    _d['L0_attn_x'] = jax.random.normal(jax.random.fold_in(jax.random.key(seed), 1), (32, 256, 128), dtype=_x0.dtype)
    del _x0
    return _d

def reference(L0_attn_x, L0_attn_w_qkv, L0_attn_b_qkv, L0_attn_w_out, L0_attn_b_out, L0_ffn_router_kernel_DE, L0_ffn_kernel_gating_EDF, L0_ffn_kernel_up_EDF, L0_ffn_kernel_down_EFD):

    def _L0_attn_ref(x, w_qkv, b_qkv, w_out, b_out):
        import jax, jax.numpy as jnp
        import numpy as np
        B, T, C, H = (2, 128, 128, 16)
        D = C // H
        EPS = 1e-06
        b, t, c = x.shape
        qkv = x @ w_qkv.T + b_qkv
        q, k, v = jnp.split(qkv, 3, axis=-1)

        def to_heads(u):
            return u.reshape(b, t, H, D).transpose(0, 2, 1, 3).astype(jnp.float32)
        q, k, v = (to_heads(q), to_heads(k), to_heads(v))
        q_prime = jax.nn.elu(q) + 1.0
        k_prime = jax.nn.elu(k) + 1.0
        kv_cumsum = jnp.cumsum(jnp.einsum('bhtd,bhte->bhtde', k_prime, v), axis=2)
        context = jnp.einsum('bhtd,bhtde->bhte', q_prime, kv_cumsum)
        norm = jnp.einsum('bhtd,bhtd->bht', q_prime, jnp.cumsum(k_prime, axis=2))
        out = context / (norm[..., None] + EPS)
        out = out.astype(x.dtype).transpose(0, 2, 1, 3).reshape(b, t, c)
        return out @ w_out.T + b_out

    def _L0_ffn_ref(x, router_kernel_DE, kernel_gating_EDF, kernel_up_EDF, kernel_down_EFD):
        import jax, jax.numpy as jnp
        import numpy as np
        TOP_K = 2
        E = router_kernel_DE.shape[-1]
        x = x.astype(jnp.float32)
        logits_BSE = jnp.einsum('BSD,DE->BSE', x, router_kernel_DE)
        probs_BSE = jax.nn.softmax(logits_BSE.astype(jnp.float32), axis=-1)
        weights_BSK, indices_BSK = jax.lax.top_k(probs_BSE, TOP_K)
        norm_weights_BSK = jax.nn.softmax(weights_BSK, axis=-1)
        one_hot_BSKE = jax.nn.one_hot(indices_BSK, num_classes=E, dtype=x.dtype)
        full_weights_BSE = jnp.sum(one_hot_BSKE * norm_weights_BSK[..., None], axis=2)
        gating_BSEF = jnp.einsum('BSD,EDF->BSEF', x, kernel_gating_EDF)
        act_BSEF = jax.nn.silu(gating_BSEF)
        up_BSEF = jnp.einsum('BSD,EDF->BSEF', x, kernel_up_EDF)
        fuse_BSEF = act_BSEF * up_BSEF
        down_BSED = jnp.einsum('BSEF,EFD->BSED', fuse_BSEF, kernel_down_EFD)
        out_BSD = jnp.einsum('BSED,BSE->BSD', down_BSED, full_weights_BSE)
        return out_BSD.astype(jnp.float32)
    x = L0_attn_x
    x = _layernorm(x + _L0_attn_ref(x, L0_attn_w_qkv, L0_attn_b_qkv, L0_attn_w_out, L0_attn_b_out), axis=-1)
    x = _layernorm(x + _L0_ffn_ref(x, L0_ffn_router_kernel_DE, L0_ffn_kernel_gating_EDF, L0_ffn_kernel_up_EDF, L0_ffn_kernel_down_EFD), axis=-1)
    return x

_drawn_inputs = setup_inputs


def setup_inputs(seed=0):
    import zlib

    import numpy as np

    out = dict(_drawn_inputs(seed))
    spreads = {}
    factors = {'L0_attn_w_qkv': 7.022,
     'L0_attn_b_qkv': 8.0,
     'L0_attn_w_out': 5.98,
     'L0_attn_b_out': 2.749,
     'L0_ffn_router_kernel_DE': 8.0,
     'L0_ffn_kernel_gating_EDF': 8.0,
     'L0_ffn_kernel_up_EDF': 8.0,
     'L0_ffn_kernel_down_EFD': 8.0}
    for name, (base, spread) in spreads.items():
        noise = np.random.default_rng([zlib.crc32(name.encode()), seed]).standard_normal(out[name].shape)
        drawn = base * np.exp(spread * noise) if base else spread * noise
        out[name] = jnp.asarray(drawn.astype(out[name].dtype))
    for name, factor in factors.items():
        out[name] = (out[name] * factor).astype(out[name].dtype)
    return out
```

```python
import concourse.bass as bass
from concourse import mybir
from contextlib import ExitStack

F32 = mybir.dt.float32
F32R = mybir.dt.float32r
I32 = mybir.dt.int32
U32 = mybir.dt.uint32
ALU = mybir.AluOpType
ACT = mybir.ActivationFunctionType
AX_X = mybir.AxisListType.X

P = 128
TILES = 4
GT = P * TILES
HEADS = 16
D = P // HEADS
HALF = P // 2 * D
EPS_NORM = 1e-6
EPS_LN = 1e-5
RSQRT_MAGIC = float(0x5F3759DF)


def wait(eng, sem, value):
    if isinstance(value, int) and value <= 0:
        return
    eng.wait_ge(sem, value)


def attn_moe_kernel(nc, x, w_qkv_t, b_qkv, w_out_t, b_out, w_router, w_gate, w_up, w_down, out):
    B, T, C = x.shape
    E, _, F = w_gate.shape
    FC = F // P
    CH = E * FC
    GROUPS = B * T // GT
    QK = 2 * C
    assert C == P and T == 2 * P and CH == 16 and E == 8 and GROUPS == 16

    x_g = x.rearrange("(g b) (j p) c -> g p (b j) c", g=GROUPS, p=P)
    out_g = out.rearrange("(g b) (j p) c -> g p (b j) c", g=GROUPS, p=P)

    with ExitStack() as ctx:
        def sb(name, shape, dt=F32):
            return ctx.enter_context(nc.sbuf_tensor(name, shape, dt))

        def bank(name):
            return ctx.enter_context(nc.psum_tensor(name, [P, GT], F32))

        def sem(name):
            return ctx.enter_context(nc.semaphore(name))

        ident = sb("ident", [P, P])
        tri_f = sb("tri_f", [P, P])
        ones_f = sb("ones_f", [P, P])
        tri = sb("tri", [P, P], F32R)
        ones = sb("ones", [P, P], F32R)
        sel_f = sb("sel_f", [64, E, P])
        sel = sb("sel", [64, E, P], F32R)
        eidx = sb("eidx", [P, TILES, E])
        b_out_bc = sb("b_out_bc", [P, C])
        c_eps = sb("c_eps", [P, TILES])
        c_mhalf = sb("c_mhalf", [P, TILES])
        c_3half = sb("c_3half", [P, TILES])
        bq_f = sb("bq_f", [64, 3 * C])
        bq = sb("bq", [64, 3 * C], F32R)

        wqkv_hi = sb("wqkv_hi", [P, 3 * C], F32R)
        wqkv_lo = sb("wqkv_lo", [P, 3 * C], F32R)
        wo_hi = sb("wo_hi", [P, C], F32R)
        wo_lo = sb("wo_lo", [P, C], F32R)
        wr_hi = sb("wr_hi", [P, E], F32R)
        wr_lo = sb("wr_lo", [P, E], F32R)
        wg_hi = sb("wg_hi", [P, E, F], F32R)
        wg_lo = sb("wg_lo", [P, E, F], F32R)
        wu_hi = sb("wu_hi", [P, E, F], F32R)
        wu_lo = sb("wu_lo", [P, E, F], F32R)
        wd_hi = sb("wd_hi", [P, CH, C], F32R)
        wd_lo = sb("wd_lo", [P, CH, C], F32R)
        stage = sb("stage", [P, 3, 2048])

        xin = sb("xin", [P, TILES, C])
        xb = sb("xb", [P, TILES, C])
        xT_hi = sb("xT_hi", [P, GT], F32R)
        xT_lo = sb("xT_lo", [P, GT], F32R)
        z = sb("z", [P, TILES, 3 * C])
        neg = sb("neg", [P, TILES, QK])
        qk = sb("qk", [P, TILES, QK])
        kk_hi = sb("kk_hi", [P, TILES, C], F32R)
        kk_lo = sb("kk_lo", [P, TILES, C], F32R)
        qn = sb("qn", [P, TILES, C])
        nrm = sb("nrm", [P, TILES * HEADS])
        nrm_e = sb("nrm_e", [P, TILES * HEADS])
        rnrm = sb("rnrm", [P, TILES * HEADS])
        qs = sb("qs", [P, TILES, C])
        pf = sb("pf", [P, 2, HALF])
        p_hi = sb("p_hi", [P, 4, HALF], F32R)
        p_lo = sb("p_lo", [P, 4, HALF], F32R)
        zz = sb("zz", [P, 2, HALF])
        ctxt = sb("ctxt", [P, TILES, C])
        cT_hi = sb("cT_hi", [P, GT], F32R)
        cT_lo = sb("cT_lo", [P, GT], F32R)
        r1 = sb("r1", [P, TILES, C])
        x1 = sb("x1", [P, 2, TILES, C])
        x1T_hi = sb("x1T_hi", [P, 2, GT], F32R)
        x1T_lo = sb("x1T_lo", [P, 2, GT], F32R)

        stats = [sb(f"stats{n}", [P, TILES, 6]) for n in range(2)]
        mv = [sb(f"mv{n}", [P, TILES, 2]) for n in range(2)]
        nh = [sb(f"nh{n}", [P, TILES]) for n in range(2)]
        nv = [sb(f"nv{n}", [P, TILES]) for n in range(2)]
        ny = [sb(f"ny{n}", [P, TILES]) for n in range(2)]
        na = [sb(f"na{n}", [P, TILES]) for n in range(2)]

        mx = sb("mx", [P, TILES])
        lg = sb("lg", [P, TILES, E])
        ex = sb("ex", [P, TILES, E])
        sm = sb("sm", [P, TILES])
        rs = sb("rs", [P, TILES])
        prob = sb("prob", [P, TILES, E])
        top = sb("top", [P, TILES, 8])
        topi = sb("topi", [P, TILES, 8], U32)
        topf = sb("topf", [P, TILES, 8])
        dlt = sb("dlt", [P, TILES])
        th = sb("th", [P, TILES])
        wk = sb("wk", [P, 2, TILES])
        oh = sb("oh", [P, 2, TILES, E])
        wf = sb("wf", [P, 3, TILES, E])
        wT = sb("wT", [64, 2, GT], F32R)

        wbc = sb("wbc", [P, 2, GT])
        s_act = stage[:, 1, 0:2 * GT].rearrange("p (n t) -> p n t", n=2)
        sw = stage[:, 1, 2 * GT:].rearrange("p (n t) -> p n t", n=2)
        hf = stage[:, 2, 0:2 * GT].rearrange("p (n t) -> p n t", n=2)
        yTs = stage[:, 2, 2 * GT:3 * GT]
        r2 = stage[:, 2, 3 * GT:].rearrange("p (j c) -> p j c", j=TILES)
        h_hi = sb("h_hi", [P, 4, GT], F32R)
        h_lo = sb("h_lo", [P, 4, GT], F32R)
        res = sb("res", [P, TILES, C])

        G = [bank("G0"), bank("G1")]
        U = [bank("U0"), bank("U1")]
        Y = bank("Y")
        C0 = bank("C0")
        C1 = bank("C1")
        M = bank("M")

        names = """w_in wgu_in wd_in b_in gp_c0 gp_const dv_ones dv_const w_hi w_lo wT0
            x_in x_T xT_hi_d xT_lo_d xb_d qkv_d z_d neg_d ex_d qk_d kk_hi_d kk_lo_d cumk_d qn_d nrm_d
            nrme_d rnrm_d qs_d prod_d p_hi_d p_lo_d cum_d zz_d ctx_d ctx_T cT_hi_d cT_lo_d proj_d res_d
            st1_d mv1_d rn1_d x1_d x1_T x1T_hi_d x1T_lo_d logit_d rmax_d lg_d rex_d rchain th_d w_T wT_hi_d
            wT_lo_d wb_d wbs_d g_d u_d silu_d sw_d h_d h_hi_d h_lo_d dn_d yT_d y_T res2_d st2_d mv2_d
            rn2_d out_d stored dve_past pool_past""".split()
        S = {n: sem(n) for n in names}
        block = ctx.enter_context(nc.Block())

        RCH = 20
        NEWTON = 15

        qkv_bank = [C1, C1, C0, C1]

        def cum_bank(hs):
            return C1 if hs % 2 == 0 else C0

        @block.sync
        def _(sp):
            sp.dma_start(stage[:, 0, 0:3 * C], w_qkv_t).then_inc(S["w_in"], 16)
            sp.dma_start(stage[:, 0, 512:512 + C], w_out_t).then_inc(S["w_in"], 16)
            sp.dma_start(stage[:, 0, 1024:1024 + E], w_router).then_inc(S["w_in"], 16)
            sp.wait_ge(S["gp_c0"], 1)
            sp.dma_start(bq_f[0:1, :], b_qkv.rearrange("(o n) -> o n", o=1)).then_inc(S["b_in"], 16)
            sp.dma_start(bq_f[32:33, :], b_qkv.rearrange("(o n) -> o n", o=1)).then_inc(S["b_in"], 16)
            sp.dma_start(b_out_bc[:], b_out.rearrange("(o n) -> o n", o=1).to_broadcast([P, C])).then_inc(S["b_in"], 16)

            def load(g):
                wait(sp, S["x_T"], g)
                wait(sp, S["xb_d"], g)
                sp.dma_start(xin[:], x_g[g]).then_inc(S["x_in"], 16)

            def store(g):
                sp.wait_ge(S["out_d"], (g + 1) * TILES)
                sp.dma_start(out_g[g], res[:]).then_inc(S["stored"], 16)

            load(0)
            sp.dma_start(stage[:, 1, :].rearrange("p (e f) -> p e f", e=E),
                         w_gate.rearrange("e c f -> c e f")).then_inc(S["wgu_in"], 16)
            sp.dma_start(stage[:, 2, :].rearrange("p (e f) -> p e f", e=E),
                         w_up.rearrange("e c f -> c e f")).then_inc(S["wgu_in"], 16)
            sp.wait_ge(S["w_lo"], 3)
            sp.dma_start(stage[:, 0, :].rearrange("p (k c) -> p k c", k=CH),
                         w_down.rearrange("e (k f) c -> f (e k) c", f=P)).then_inc(S["wd_in"], 16)
            for g in (1, 2, 3):
                load(g)
            store(0)
            with sp.Fori(2, GROUPS - 2) as u:
                load(u + 2)
                store(u - 1)
            for g in range(GROUPS - 3, GROUPS):
                store(g)
            sp.wait_ge(S["stored"], 16 * GROUPS)

        @block.tensor
        def _(pe):
            mm = nc.tensor.matmul

            def three(dst, a_hi, a_lo, b_hi, b_lo, start=True, stop=True):
                mm(dst, a_hi, b_hi, start=start, stop=False)
                mm(dst, a_hi, b_lo, start=False, stop=False)
                return mm(dst, a_lo, b_hi, start=False, stop=stop)

            def transpose_x(h):
                wait(pe, S["x_in"], 16 * (h + 1))
                wait(pe, S["zz_d"], 8 * h - 1)
                for j in range(TILES):
                    last = nc.tensor.transpose(C1[:, j * P:(j + 1) * P], xin[:, j, :], ident[:])
                last.then_inc(S["x_T"], 1)

            def project(h, j, tail):
                if j == 0:
                    pe.wait_ge(S["xT_hi_d"], h + 1)
                    pe.wait_ge(S["xT_lo_d"], h + 1)
                elif j != 2:
                    pe.wait_ge(S["z_d"], 4 * h + (1 if j == 1 else 2))
                elif tail is not None:
                    pe.wait_ge(S["res_d"], tail + 1)
                dst = qkv_bank[j][:, 0:3 * C]
                cols = slice(j * P, (j + 1) * P)
                mm(dst, xT_hi[:, cols], wqkv_hi[:], start=True, stop=False)
                mm(dst, xT_hi[:, cols], wqkv_lo[:], start=False, stop=False)
                mm(dst, xT_lo[:, cols], wqkv_hi[:], start=False, stop=False)
                mm(dst, ones[0:64, :], bq[:], start=False, stop=True).then_inc(S["qkv_d"], 1)

            def cumulate_k(h, y):
                pe.wait_ge(S["kk_hi_d"], h + 1)
                pe.wait_ge(S["kk_lo_d"], h + 1)
                if y is not None:
                    pe.wait_ge(S["res2_d"], y + 1)
                else:
                    pe.wait_ge(S["z_d"], 4 * h + 3)
                mm(C0[:], tri[:], kk_hi[:].rearrange("p j c -> p (j c)"), start=True, stop=False)
                mm(C0[:], tri[:], kk_lo[:].rearrange("p j c -> p (j c)"), start=False, stop=False)
                second = C0[:].rearrange("p (b j c) -> p b j c", b=2, j=2)[:, :, 1, :]
                mm(second, ones[:], kk_hi[:].rearrange("p (b j) c -> p b j c", b=2)[:, :, 0, :],
                   start=False, stop=False)
                mm(second, ones[:], kk_lo[:].rearrange("p (b j) c -> p b j c", b=2)[:, :, 0, :],
                   start=False, stop=True).then_inc(S["cumk_d"], 1)

            def cumulate(h, hs, tail):
                pe.wait_ge(S["p_hi_d"], 8 * h + hs + 1)
                pe.wait_ge(S["p_lo_d"], 8 * h + hs + 1)
                if hs == 0:
                    if tail is not None:
                        pe.wait_ge(S["lg_d"], tail + 1)
                    else:
                        pe.wait_ge(S["z_d"], 4 * h + 4)
                elif hs == 1:
                    pe.wait_ge(S["qn_d"], h + 1)
                else:
                    pe.wait_ge(S["zz_d"], 8 * h + hs - 1)
                dst = cum_bank(hs)
                second = (hs // 2) % 2 == 1
                mm(dst[:], tri[:], p_hi[:, hs % 4, :], start=True, stop=False)
                last = mm(dst[:], tri[:], p_lo[:, hs % 4, :], start=False, stop=not second)
                if second:
                    mm(dst[:], ones[:], p_hi[:, (hs - 2) % 4, :], start=False, stop=False)
                    last = mm(dst[:], ones[:], p_lo[:, (hs - 2) % 4, :], start=False, stop=True)
                last.then_inc(S["cum_d"], 1)

            def transpose_ctx(t):
                pe.wait_ge(S["ctx_d"], 8 * (t + 1))
                for j in range(TILES):
                    last = nc.tensor.transpose(C0[:, j * P:(j + 1) * P], ctxt[:, j, :], ident[:])
                last.then_inc(S["ctx_T"], 1)

            def out_project(t):
                pe.wait_ge(S["cT_hi_d"], t + 1)
                pe.wait_ge(S["cT_lo_d"], t + 1)
                for j in range(TILES):
                    cols = slice(j * P, (j + 1) * P)
                    last = three(C0[:, cols], cT_hi[:, cols], cT_lo[:, cols], wo_hi[:], wo_lo[:])
                last.then_inc(S["proj_d"], 1)

            def transpose_x1(t, par, head):
                pe.wait_ge(S["x1_d"], TILES * (t + 1))
                if head is not None:
                    pe.wait_ge(S["z_d"], 4 * head + 4)
                else:
                    pe.wait_ge(S["zz_d"], 8 * t + 7)
                for j in range(TILES):
                    last = nc.tensor.transpose(C1[:, j * P:(j + 1) * P], x1[:, par, j, :], ident[:])
                last.then_inc(S["x1_T"], 1)

            def logits(t, par):
                pe.wait_ge(S["x1T_hi_d"], t + 1)
                pe.wait_ge(S["x1T_lo_d"], t + 1)
                for j in range(TILES):
                    cols = slice(j * P, (j + 1) * P)
                    last = three(C1[:, j * E:(j + 1) * E], x1T_hi[:, par, cols], x1T_lo[:, par, cols],
                                 wr_hi[:], wr_lo[:])
                last.then_inc(S["logit_d"], 1)

            def transpose_w(t, moe):
                pe.wait_ge(S["rchain"], RCH * (t + 1))
                if moe is not None:
                    pe.wait_ge(S["wbs_d"], E * moe + E - 1)
                for j in range(TILES):
                    last = nc.tensor.transpose(M[0:E, j * P:(j + 1) * P], wf[:, 2, j, :], ident[:])
                last.then_inc(S["w_T"], 1)

            def transpose_y(y, tail, head):
                pe.wait_ge(S["yT_d"], y + 1)
                if head is not None:
                    pe.wait_ge(S["z_d"], 4 * head + 3)
                elif tail is not None:
                    pe.wait_ge(S["res_d"], tail + 1)
                else:
                    wait(pe, S["res2_d"], y)
                for j in range(TILES):
                    last = nc.tensor.transpose(C0[:, j * P:(j + 1) * P], yTs[:, j * P:(j + 1) * P], ident[:])
                last.then_inc(S["y_T"], 1)

            def spread(m, par, e, tail):
                if e == 0:
                    pe.wait_ge(S["wT_hi_d"], m + 1)
                    pe.wait_ge(S["wT_lo_d"], m + 1)
                    wait(pe, S["wbs_d"], E * m)
                elif e == E - 1 and tail is not None:
                    pe.wait_ge(S["wT_hi_d"], tail + 1)
                    pe.wait_ge(S["wT_lo_d"], tail + 1)
                else:
                    pe.wait_ge(S["wbs_d"], E * m + e)
                mm(M[:], sel[:, e, :], wT[:, par, :], start=True, stop=True).then_inc(S["wb_d"], 1)

            def gate_up(m, par, k):
                n = CH * m + k
                if k == 0:
                    pe.wait_ge(S["x1T_hi_d"], m + 1)
                    pe.wait_ge(S["x1T_lo_d"], m + 1)
                e, f = k // FC, slice(k % FC * P, (k % FC + 1) * P)
                wait(pe, S["silu_d"], n - 1)
                three(G[k % 2][:], wg_hi[:, e, f], wg_lo[:, e, f], x1T_hi[:, par, :],
                      x1T_lo[:, par, :]).then_inc(S["g_d"], 1)
                wait(pe, S["h_d"], n - 1)
                three(U[k % 2][:], wu_hi[:, e, f], wu_lo[:, e, f], x1T_hi[:, par, :],
                      x1T_lo[:, par, :]).then_inc(S["u_d"], 1)

            def down(m, k):
                n = CH * m + k
                pe.wait_ge(S["h_hi_d"], n + 1)
                pe.wait_ge(S["h_lo_d"], n + 1)
                if k == 0:
                    wait(pe, S["yT_d"], m)
                three(Y[:], wd_hi[:, k, :], wd_lo[:, k, :], h_hi[:, k % 4, :], h_lo[:, k % 4, :],
                      start=(k == 0), stop=(k == CH - 1)).then_inc(S["dn_d"], 1)

            def step(s, m, par, tail, head, y):
                if s == 0:
                    if head is not None:
                        transpose_x(head)
                    if tail is not None:
                        transpose_ctx(tail)
                if s == 1:
                    if tail is not None:
                        out_project(tail)
                    if head is not None:
                        project(head, 0, tail)
                if s == 2 and head is not None:
                    project(head, 1, tail)
                    project(head, 2, tail)
                if s == 3:
                    if head is not None:
                        project(head, 3, tail)
                    if y is not None:
                        transpose_y(y, tail, head)
                if s == 4 and tail is not None:
                    transpose_x1(tail, 1 - par, head)
                if s == 5 and tail is not None:
                    logits(tail, 1 - par)
                if s == 6 and head is not None:
                    cumulate_k(head, y)
                if 7 <= s <= 14 and head is not None:
                    cumulate(head, s - 7, tail)
                if s == 13 and tail is not None:
                    transpose_w(tail, m)

            def unit(m, par, tail, head, y):
                for s in range(CH):
                    if m is not None:
                        if s % FC == 0:
                            spread(m, par, s // FC, tail)
                        gate_up(m, par, s)
                        if s >= 2:
                            down(m, s - 2)
                    if m is not None and y is not None and s < 2:
                        down(y, CH - 2 + s)
                    step(s, m, par, tail, head, y)

            pe.wait_ge(S["gp_const"], 3)
            pe.wait_ge(S["dv_const"], 3)
            pe.wait_ge(S["w_hi"], 4)
            pe.wait_ge(S["w_lo"], 4)
            unit(None, 0, None, 0, None)
            unit(None, 1, 0, 1, None)
            pe.wait_ge(S["wT0"], 1)
            pe.wait_ge(S["w_hi"], 7)
            pe.wait_ge(S["w_lo"], 7)
            unit(0, 0, 1, 2, None)
            with pe.Fori(1, GROUPS - 3, 2) as u:
                unit(u, 1, u + 1, u + 2, u - 1)
                unit(u + 1, 0, u + 2, u + 3, u)
            unit(GROUPS - 3, 1, GROUPS - 2, GROUPS - 1, GROUPS - 4)
            unit(GROUPS - 2, 0, GROUPS - 1, None, GROUPS - 3)
            unit(GROUPS - 1, 1, None, None, GROUPS - 2)
            down(GROUPS - 1, CH - 2)
            down(GROUPS - 1, CH - 1)
            transpose_y(GROUPS - 1, None, None)

        @block.scalar
        def _(act):
            def copy(dst, src):
                return nc.scalar.activation(dst, src, ACT.Copy)

            def z_copy(h, j):
                act.wait_ge(S["qkv_d"], 4 * h + j + 1)
                if j == 0:
                    wait(act, S["qk_d"], h)
                    wait(act, S["prod_d"], 8 * h)
                copy(z[:, j, :], qkv_bank[j][:, 0:3 * C]).then_inc(S["z_d"], 1)

            def product_hi(h, hs):
                act.wait_ge(S["prod_d"], 8 * h + hs + 1)
                wait(act, S["cum_d"], 8 * h + hs - 1)
                copy(p_hi[:, hs % 4, :], pf[:, hs % 2, :]).then_inc(S["p_hi_d"], 1)

            def silu(m, k):
                n = CH * m + k
                act.wait_ge(S["g_d"], n + 1)
                wait(act, S["sw_d"], n - 1)
                nc.scalar.activation(s_act[:, k % 2, :], G[k % 2][:], ACT.Silu).then_inc(S["silu_d"], 1)

            def hidden_hi(m, k):
                n = CH * m + k
                act.wait_ge(S["h_d"], n + 1)
                wait(act, S["dn_d"], n - 3)
                copy(h_hi[:, k % 4, :], hf[:, k % 2, :]).then_inc(S["h_hi_d"], 1)

            def weights_out(m, e):
                act.wait_ge(S["wb_d"], E * m + e + 1)
                wait(act, S["sw_d"], CH * m + FC * (e - 1))
                copy(wbc[:, e % 2, :], M[:]).then_inc(S["wbs_d"], 1)

            def step(s, m, par, tail, head, y):
                if s == 0:
                    if head is not None:
                        act.wait_ge(S["x_T"], head + 1)
                        wait(act, S["qkv_d"], 4 * head)
                        copy(xT_hi[:], C1[:]).then_inc(S["xT_hi_d"], 1)
                    if tail is not None:
                        act.wait_ge(S["ctx_T"], tail + 1)
                        wait(act, S["proj_d"], tail)
                        copy(cT_hi[:], C0[:]).then_inc(S["cT_hi_d"], 1)
                if s == 1:
                    if y is not None:
                        act.wait_ge(S["dn_d"], CH * (y + 1))
                        wait(act, S["y_T"], y)
                        copy(yTs, Y[:]).then_inc(S["yT_d"], 1)
                    if head is not None:
                        z_copy(head, 0)
                if s == 2 and head is not None:
                    z_copy(head, 1)
                    z_copy(head, 2)
                if s == 3 and head is not None:
                    z_copy(head, 3)
                if s == 4 and tail is not None:
                    act.wait_ge(S["x1_T"], tail + 1)
                    if not isinstance(tail, int) or tail >= 2:
                        act.wait_ge(S["u_d"], CH * (tail - 1))
                        act.wait_ge(S["logit_d"], tail)
                    copy(x1T_hi[:, 1 - par, :], C1[:]).then_inc(S["x1T_hi_d"], 1)
                if s == 5 and head is not None:
                    act.wait_ge(S["neg_d"], head + 1)
                    nc.scalar.activation(neg[:], neg[:], ACT.Exp).then_inc(S["ex_d"], 1)
                if s == 6:
                    if tail is not None:
                        act.wait_ge(S["lg_d"], tail + 1)
                        wait(act, S["rchain"], RCH * tail)
                        nc.scalar.activation(ex[:], lg[:], ACT.Exp).then_inc(S["rex_d"], 1)
                    if head is not None:
                        act.wait_ge(S["qk_d"], head + 1)
                        wait(act, S["cumk_d"], head)
                        copy(kk_hi[:], qk[:, :, C:QK]).then_inc(S["kk_hi_d"], 1)
                if 7 <= s <= 14 and head is not None:
                    product_hi(head, s - 7)
                if s == 10 and tail is not None:
                    act.wait_ge(S["rchain"], RCH * tail + 12)
                    nc.scalar.activation(th[:], dlt[:], ACT.Tanh, scale=0.5).then_inc(S["th_d"], 1)
                if s == 13 and tail is not None:
                    act.wait_ge(S["w_T"], tail + 1)
                    wait(act, S["wb_d"], E * (tail - 1))
                    copy(wT[0:E, 1 - par, :], M[0:E, :]).then_inc(S["wT_hi_d"], 1)

            def unit(m, par, tail, head, y):
                for s in range(CH):
                    if m is not None:
                        if s % FC == 0:
                            weights_out(m, s // FC)
                        silu(m, s)
                        if s >= 1:
                            hidden_hi(m, s - 1)
                        elif y is not None:
                            hidden_hi(y, CH - 1)
                    step(s, m, par, tail, head, y)

            act.wait_ge(S["w_in"], 48)
            copy(wqkv_hi[:], stage[:, 0, 0:3 * C]).then_inc(S["w_hi"], 1)
            copy(wo_hi[:], stage[:, 0, 512:512 + C]).then_inc(S["w_hi"], 1)
            copy(wr_hi[:], stage[:, 0, 1024:1024 + E]).then_inc(S["w_hi"], 1)
            act.wait_ge(S["b_in"], 48)
            copy(bq[0:32, :], bq_f[0:32, :]).then_inc(S["w_hi"], 1)
            unit(None, 0, None, 0, None)
            act.wait_ge(S["wgu_in"], 32)
            act.wait_ge(S["wd_in"], 16)
            copy(wg_hi[:].rearrange("p e f -> p (e f)"), stage[:, 1, :]).then_inc(S["w_hi"], 1)
            copy(wu_hi[:].rearrange("p e f -> p (e f)"), stage[:, 2, :]).then_inc(S["w_hi"], 1)
            copy(wd_hi[:].rearrange("p k c -> p (k c)"), stage[:, 0, :]).then_inc(S["w_hi"], 1)
            unit(None, 1, 0, 1, None)
            unit(0, 0, 1, 2, None)
            with act.Fori(1, GROUPS - 3, 2) as u:
                unit(u, 1, u + 1, u + 2, u - 1)
                unit(u + 1, 0, u + 2, u + 3, u)
            unit(GROUPS - 3, 1, GROUPS - 2, GROUPS - 1, GROUPS - 4)
            unit(GROUPS - 2, 0, GROUPS - 1, None, GROUPS - 3)
            unit(GROUPS - 1, 1, None, None, GROUPS - 2)
            hidden_hi(GROUPS - 1, CH - 1)
            act.wait_ge(S["dn_d"], CH * GROUPS)
            act.wait_ge(S["y_T"], GROUPS - 1)
            copy(yTs, Y[:]).then_inc(S["yT_d"], 1)

        @block.vector
        def _(dve):
            tt = nc.vector.tensor_tensor
            ts = nc.vector.tensor_scalar

            def low(dst, src, hi):
                return tt(dst, src, hi.bitcast(F32), ALU.subtract)

            def hidden(m, k):
                n = CH * m + k
                dve.wait_ge(S["sw_d"], n + 1)
                dve.wait_ge(S["u_d"], n + 1)
                wait(dve, S["h_hi_d"], n - 1)
                wait(dve, S["h_lo_d"], n - 1)
                tt(hf[:, k % 2, :], U[k % 2][:], sw[:, k % 2, :], ALU.mult).then_inc(S["h_d"], 1)

            def hidden_lo(m, k):
                n = CH * m + k
                dve.wait_ge(S["h_hi_d"], n + 1)
                wait(dve, S["dn_d"], n - 3)
                low(h_lo[:, k % 4, :], hf[:, k % 2, :], h_hi[:, k % 4, :]).then_inc(S["h_lo_d"], 1)

            def statistics(n, g, src):
                st, mvs = S[f"st{n + 1}_d"], S[f"mv{n + 1}_d"]
                wait(dve, mvs, TILES * g)
                for j in range(TILES):
                    nc.vector.bn_stats(stats[n][:, j, :], src[:, j, :]).then_inc(st, 1)
                wait(dve, S["x1_d"] if n == 0 else S["out_d"], TILES * g)
                dve.wait_ge(st, TILES * (g + 1))
                dve.sem_inc(S["dve_past"], 1)
                for j in range(TILES):
                    nc.vector.bn_aggr(mv[n][:, j, :], stats[n][:, j, :]).then_inc(mvs, 1)

            def half_product_lo(h, hs):
                dve.wait_ge(S["p_hi_d"], 8 * h + hs + 1)
                wait(dve, S["cum_d"], 8 * h + hs - 1)
                low(p_lo[:, hs % 4, :], pf[:, hs % 2, :], p_hi[:, hs % 4, :]).then_inc(S["p_lo_d"], 1)

            def apply_q(h, hs):
                j, half = hs // 2, hs % 2
                dve.wait_ge(S["cum_d"], 8 * h + hs + 1)
                dve.wait_ge(S["qs_d"], h + 1)
                wait(dve, S["ctx_d"], 8 * h + hs - 1)
                q4 = qs[:, j, half * 64:(half + 1) * 64].rearrange("p (h o d) -> p h o d", o=1, d=D)
                tt(zz[:, hs % 2, :].rearrange("p (h e d) -> p h e d", e=D, d=D),
                   cum_bank(hs)[:].rearrange("p (h e d) -> p h e d", e=D, d=D),
                   q4.to_broadcast([P, HEADS // 2, D, D]), ALU.mult).then_inc(S["zz_d"], 1)

            def contract(h, hs):
                j, half = hs // 2, hs % 2
                dve.wait_ge(S["zz_d"], 8 * h + hs + 1)
                wait(dve, S["ctx_T"], h)
                nc.vector.tensor_reduce(ctxt[:, j, half * 64:(half + 1) * 64],
                                        zz[:, hs % 2, :].rearrange("p (c d) -> p c d", d=D),
                                        AX_X, ALU.add).then_inc(S["ctx_d"], 1)

            def bc(v):
                return v.rearrange("p (j o) -> p j o", o=1).to_broadcast([P, TILES, E])

            def router(t, a, b):
                base = RCH * t
                c = S["rchain"]

                def after(n):
                    wait(dve, c, base + n)
                done = 0
                def s1():
                    dve.wait_ge(S["rex_d"], t + 1)
                    return nc.vector.tensor_reduce(sm[:], ex[:], AX_X, ALU.add)
                def s2():
                    after(1)
                    return nc.vector.reciprocal(rs[:], sm[:])
                def s3():
                    after(2)
                    return tt(prob[:], ex[:], bc(rs[:]), ALU.mult)
                def s_max(j):
                    def s():
                        if j == 0:
                            after(3)
                            dve.sem_inc(S["dve_past"], 1)
                        return nc.vector.max(top[:, j, :], prob[:, j, :])
                    return s
                def s_idx(j):
                    def s():
                        if j == 0:
                            after(7)
                            dve.sem_inc(S["dve_past"], 1)
                        return nc.vector.max_index(topi[:, j, :], top[:, j, :], prob[:, j, :])
                    return s
                def s12():
                    after(7)
                    wait(dve, S["th_d"], t)
                    return tt(dlt[:], top[:, :, 0], top[:, :, 1], ALU.subtract)
                def s13():
                    after(11)
                    return nc.vector.tensor_copy(topf[:], topi[:])
                def s14():
                    dve.wait_ge(S["th_d"], t + 1)
                    return ts(wk[:, 0, :], th[:], 0.5, 0.5, ALU.mult, ALU.add)
                def s15():
                    return ts(wk[:, 1, :], th[:], -0.5, 0.5, ALU.mult, ALU.add)
                def s_oh(n):
                    def s():
                        after(13)
                        return tt(oh[:, n], eidx[:], bc(topf[:, :, n]), ALU.is_equal)
                    return s
                def s_w(n):
                    def s():
                        after(16 + n)
                        return tt(wf[:, n], oh[:, n], bc(wk[:, n, :]), ALU.mult)
                    return s
                def s20():
                    after(19)
                    wait(dve, S["w_T"], t)
                    return tt(wf[:, 2], wf[:, 0], wf[:, 1], ALU.add)
                steps = ([s1, s2, s3] + [s_max(j) for j in range(TILES)] + [s_idx(j) for j in range(TILES)]
                         + [s12, s13, s14, s15, s_oh(0), s_oh(1), s_w(0), s_w(1), s20])
                for n in range(a, b + 1):
                    steps[n - 1]().then_inc(c, 1)

            def step(s, m, par, tail, head, y):
                if s == 0:
                    if head is not None:
                        dve.wait_ge(S["xT_hi_d"], head + 1)
                        wait(dve, S["qkv_d"], 4 * head)
                        low(xT_lo[:], C1[:], xT_hi[:]).then_inc(S["xT_lo_d"], 1)
                    if tail is not None:
                        dve.wait_ge(S["cT_hi_d"], tail + 1)
                        wait(dve, S["proj_d"], tail)
                        low(cT_lo[:], C0[:], cT_hi[:]).then_inc(S["cT_lo_d"], 1)
                if s == 1 and tail is not None:
                    dve.wait_ge(S["proj_d"], tail + 1)
                    dve.wait_ge(S["xb_d"], tail + 1)
                    wait(dve, S["x1_d"], TILES * tail)
                    tt(r1[:].rearrange("p j c -> p (j c)"), C0[:], xb[:].rearrange("p j c -> p (j c)"),
                       ALU.add).then_inc(S["res_d"], 1)
                    dve.wait_ge(S["res_d"], tail + 1)
                    statistics(0, tail, r1)
                if s == 3 and y is not None:
                    dve.wait_ge(S["y_T"], y + 1)
                    wait(dve, S["out_d"], TILES * y)
                    tt(r2.rearrange("p j c -> p (j c)"), C0[:],
                       x1[:, 1 - par, :, :].rearrange("p j c -> p (j c)"), ALU.add).then_inc(S["res2_d"], 1)
                    dve.wait_ge(S["res2_d"], y + 1)
                    statistics(1, y, r2)
                if s == 4:
                    if head is not None:
                        dve.wait_ge(S["z_d"], 4 * head + 4)
                        wait(dve, S["qk_d"], head)
                        ts(neg[:], z[:, :, 0:QK], 0.0, None, ALU.min).then_inc(S["neg_d"], 1)
                    if tail is not None:
                        dve.wait_ge(S["x1T_hi_d"], tail + 1)
                        if not isinstance(tail, int) or tail >= 2:
                            dve.wait_ge(S["u_d"], CH * (tail - 1))
                            dve.wait_ge(S["logit_d"], tail)
                        low(x1T_lo[:, 1 - par, :], C1[:], x1T_hi[:, 1 - par, :]).then_inc(S["x1T_lo_d"], 1)
                if s == 5:
                    if tail is not None:
                        dve.wait_ge(S["logit_d"], tail + 1)
                        lg3 = C1[:, 0:TILES * E].rearrange("p (j e) -> p j e", e=E)
                        wait(dve, S["lg_d"], tail)
                        nc.vector.tensor_reduce(mx[:], lg3, AX_X, ALU.max).then_inc(S["rmax_d"], 1)
                        dve.wait_ge(S["rmax_d"], tail + 1)
                        wait(dve, S["rex_d"], tail)
                        tt(lg[:], lg3, bc(mx[:]), ALU.subtract).then_inc(S["lg_d"], 1)
                    if head is not None:
                        dve.wait_ge(S["ex_d"], head + 1)
                        wait(dve, S["qs_d"], head)
                        wait(dve, S["kk_lo_d"], head)
                        wait(dve, S["prod_d"], 8 * head)
                        wait(dve, S["kk_hi_d"], head)
                        nc.vector.scalar_tensor_tensor(out=qk[:], in0=z[:, :, 0:QK], scalar=0.0, in1=neg[:],
                                                       op0=ALU.max, op1=ALU.add).then_inc(S["qk_d"], 1)
                if s == 6 and head is not None:
                    dve.wait_ge(S["kk_hi_d"], head + 1)
                    wait(dve, S["cumk_d"], head)
                    low(kk_lo[:], qk[:, :, C:QK], kk_hi[:]).then_inc(S["kk_lo_d"], 1)
                    dve.wait_ge(S["cumk_d"], head + 1)
                    wait(dve, S["nrm_d"], head)
                    tt(qn[:].rearrange("p j c -> p j c"), C0[:].rearrange("p (j c) -> p j c", c=C),
                       qk[:, :, 0:C], ALU.mult).then_inc(S["qn_d"], 1)
                    dve.wait_ge(S["qn_d"], head + 1)
                    nc.vector.tensor_reduce(nrm[:], qn[:].rearrange("p j (h d) -> p (j h) d", d=D),
                                            AX_X, ALU.add).then_inc(S["nrm_d"], 1)
                    dve.wait_ge(S["nrm_d"], head + 1)
                    ts(nrm_e[:], nrm[:], EPS_NORM, None, ALU.add).then_inc(S["nrme_d"], 1)
                    dve.wait_ge(S["nrme_d"], head + 1)
                    nc.vector.reciprocal(rnrm[:], nrm_e[:]).then_inc(S["rnrm_d"], 1)
                    dve.wait_ge(S["rnrm_d"], head + 1)
                    wait(dve, S["zz_d"], 8 * head)
                    tt(qs[:].rearrange("p j (h d) -> p j h d", d=D),
                       qk[:, :, 0:C].rearrange("p j (h d) -> p j h d", d=D),
                       rnrm[:].rearrange("p (j h o) -> p j h o", o=1, h=HEADS).to_broadcast([P, TILES, HEADS, D]),
                       ALU.mult).then_inc(S["qs_d"], 1)
                if s == 14 and tail is not None:
                    dve.wait_ge(S["wT_hi_d"], tail + 1)
                    wait(dve, S["wb_d"], E * (tail - 1))
                    low(wT[32:32 + E, 1 - par, :], M[0:E, :], wT[0:E, 1 - par, :]).then_inc(S["wT_lo_d"], 1)
                if head is not None:
                    if 7 <= s <= 14:
                        half_product_lo(head, s - 7)
                    if 8 <= s <= 15:
                        apply_q(head, s - 8)
                        contract(head, s - 8)
                if tail is not None:
                    if s == 7:
                        router(tail, 1, 3)
                    if s == 8:
                        router(tail, 4, 11)
                    if s == 9:
                        router(tail, 12, 13)
                    if s == 11:
                        router(tail, 14, 17)
                    if s == 12:
                        router(tail, 18, 20)

            def unit(m, par, tail, head, y):
                for s in range(CH):
                    if m is not None:
                        if s >= 1:
                            hidden(m, s - 1)
                        elif y is not None:
                            hidden(y, CH - 1)
                    step(s, m, par, tail, head, y)
                    if m is not None:
                        if s >= 1:
                            hidden_lo(m, s - 1)
                        elif y is not None:
                            hidden_lo(y, CH - 1)

            dve.wait_ge(S["gp_const"], 3)
            nc.vector.tensor_copy(tri[:], tri_f[:]).then_inc(S["dv_const"], 1)
            nc.vector.tensor_copy(ones[:], ones_f[:]).then_inc(S["dv_const"], 1)
            nc.vector.tensor_copy(sel[:].rearrange("p e c -> p (e c)"),
                                  sel_f[:].rearrange("p e c -> p (e c)")).then_inc(S["dv_const"], 1)
            nc.vector.memset(wT[:].bitcast(F32), 0.0).then_inc(S["wT0"], 1)
            dve.wait_ge(S["wT0"], 1)
            dve.wait_ge(S["w_hi"], 4)
            low(wqkv_lo[:], stage[:, 0, 0:3 * C], wqkv_hi[:]).then_inc(S["w_lo"], 1)
            low(wo_lo[:], stage[:, 0, 512:512 + C], wo_hi[:]).then_inc(S["w_lo"], 1)
            low(wr_lo[:], stage[:, 0, 1024:1024 + E], wr_hi[:]).then_inc(S["w_lo"], 1)
            low(bq[32:64, :], bq_f[0:32, :], bq[0:32, :]).then_inc(S["w_lo"], 1)
            unit(None, 0, None, 0, None)
            dve.wait_ge(S["w_hi"], 7)
            low(wg_lo[:].rearrange("p e f -> p (e f)"), stage[:, 1, :],
                wg_hi[:].rearrange("p e f -> p (e f)")).then_inc(S["w_lo"], 1)
            low(wu_lo[:].rearrange("p e f -> p (e f)"), stage[:, 2, :],
                wu_hi[:].rearrange("p e f -> p (e f)")).then_inc(S["w_lo"], 1)
            low(wd_lo[:].rearrange("p k c -> p (k c)"), stage[:, 0, :],
                wd_hi[:].rearrange("p k c -> p (k c)")).then_inc(S["w_lo"], 1)
            unit(None, 1, 0, 1, None)
            unit(0, 0, 1, 2, None)
            with dve.Fori(1, GROUPS - 3, 2) as u:
                unit(u, 1, u + 1, u + 2, u - 1)
                unit(u + 1, 0, u + 2, u + 3, u)
            unit(GROUPS - 3, 1, GROUPS - 2, GROUPS - 1, GROUPS - 4)
            unit(GROUPS - 2, 0, GROUPS - 1, None, GROUPS - 3)
            unit(GROUPS - 1, 1, None, None, GROUPS - 2)
            hidden(GROUPS - 1, CH - 1)
            hidden_lo(GROUPS - 1, CH - 1)
            step(3, None, 0, None, None, GROUPS - 1)

        @block.gpsimd
        def _(pool):
            gtt = nc.gpsimd.tensor_tensor
            gts = nc.gpsimd.tensor_scalar

            def weigh(m, k):
                n = CH * m + k
                pool.wait_ge(S["silu_d"], n + 1)
                pool.wait_ge(S["wbs_d"], E * m + k // FC + 1)
                wait(pool, S["h_d"], n - 1)
                gtt(sw[:, k % 2, :], s_act[:, k % 2, :], wbc[:, (k // FC) % 2, :], ALU.mult).then_inc(S["sw_d"], 1)

            def half_product(h, hs):
                j, half = hs // 2, hs % 2
                if hs == 0:
                    pool.wait_ge(S["qk_d"], h + 1)
                wait(pool, S["p_hi_d"], 8 * h + hs - 1)
                wait(pool, S["p_lo_d"], 8 * h + hs - 1)
                k0, v0 = C + half * 64, QK + half * 64
                k4 = qk[:, j, k0:k0 + 64].rearrange("p (h o d) -> p h o d", o=1, d=D)
                v4 = z[:, j, v0:v0 + 64].rearrange("p (h e o) -> p h e o", o=1, e=D)
                shape = [P, HEADS // 2, D, D]
                gtt(pf[:, hs % 2, :].rearrange("p (h e d) -> p h e d", e=D, d=D), k4.to_broadcast(shape),
                    v4.to_broadcast(shape), ALU.mult).then_inc(S["prod_d"], 1)

            def rsqrt(n, g):
                pool.wait_ge(S[f"mv{n + 1}_d"], TILES * (g + 1))
                c = S[f"rn{n + 1}_d"]
                v, vh, y, a = nv[n][:], nh[n][:], ny[n][:], na[n][:]
                base = NEWTON * g
                wait(pool, S["x1_d"] if n == 0 else S["out_d"], TILES * g)
                gtt(v, mv[n][:, :, 1], c_eps[:], ALU.add).then_inc(c, 1)
                pool.wait_ge(c, base + 1)
                gtt(vh, v, c_mhalf[:], ALU.mult).then_inc(c, 1)
                gts(y.bitcast(I32), v.bitcast(I32), -0.5, RSQRT_MAGIC, ALU.mult, ALU.add).then_inc(c, 1)
                at = 3
                for _ in range(3):
                    pool.wait_ge(c, base + at)
                    gtt(a, y, y, ALU.mult).then_inc(c, 1)
                    pool.wait_ge(c, base + at + 1)
                    gtt(a, a, vh, ALU.mult).then_inc(c, 1)
                    pool.wait_ge(c, base + at + 2)
                    gtt(a, a, c_3half[:], ALU.add).then_inc(c, 1)
                    pool.wait_ge(c, base + at + 3)
                    gtt(y, y, a, ALU.mult).then_inc(c, 1)
                    at += 4

            def normalize(n, g, src, dst):
                y = ny[n][:]
                pool.wait_ge(S[f"rn{n + 1}_d"], NEWTON * (g + 1))
                pool.sem_inc(S["pool_past"], 1)
                for j in range(TILES):
                    gts(dst[:, j, :], src[:, j, :], mv[n][:, j, 0:1], y[:, j:j + 1], ALU.subtract,
                        ALU.mult).then_inc(S["x1_d"] if n == 0 else S["out_d"], 1)

            def step(s, m, par, tail, head, y):
                if s == 1 and tail is not None:
                    rsqrt(0, tail)
                if s == 3 and tail is not None:
                    wait(pool, S["x1_T"], tail - 1)
                    if not isinstance(tail, int) or tail >= 2:
                        pool.wait_ge(S["res2_d"], tail - 1)
                    normalize(0, tail, r1, x1[:, 1 - par])
                if s == 2 and head is not None:
                    pool.wait_ge(S["x_in"], 16 * (head + 1))
                    wait(pool, S["res_d"], head)
                    gtt(xb[:], xin[:], b_out_bc[:].rearrange("p (o c) -> p o c", o=1)
                        .to_broadcast([P, TILES, C]), ALU.add).then_inc(S["xb_d"], 1)
                if s == 4 and y is not None:
                    wait(pool, S["stored"], 16 * y)
                    rsqrt(1, y)
                    normalize(1, y, r2, res)
                if 6 <= s <= 13 and head is not None:
                    half_product(head, s - 6)

            def unit(m, par, tail, head, y):
                for s in range(CH):
                    if m is not None:
                        if s >= 1:
                            weigh(m, s - 1)
                        elif y is not None:
                            weigh(y, CH - 1)
                    step(s, m, par, tail, head, y)

            nc.gpsimd.memset(bq_f[:], 0.0).then_inc(S["gp_c0"], 1)
            nc.gpsimd.memset(ident[:], 0.0).then_inc(S["gp_c0"], 1)
            nc.gpsimd.memset(tri_f[:], 1.0).then_inc(S["gp_c0"], 1)
            nc.gpsimd.memset(sel_f[:], 0.0).then_inc(S["gp_c0"], 1)
            nc.gpsimd.memset(ones_f[:], 1.0).then_inc(S["gp_c0"], 1)
            nc.gpsimd.iota(eidx[:], pattern=[[0, TILES], [1, E]], base=0, channel_multiplier=0,
                           allow_small_or_imprecise_dtypes=True).then_inc(S["gp_c0"], 1)
            nc.gpsimd.memset(c_eps[:], EPS_LN).then_inc(S["gp_c0"], 1)
            nc.gpsimd.memset(c_mhalf[:], -0.5).then_inc(S["gp_c0"], 1)
            nc.gpsimd.memset(c_3half[:], 1.5).then_inc(S["gp_c0"], 1)
            pool.wait_ge(S["gp_c0"], 9)
            nc.gpsimd.affine_select(out=sel_f[:], in_=sel_f[:], compare_op=ALU.not_equal, fill=1.0, base=0,
                                    pattern=[[-1, E], [0, P]], channel_multiplier=1).then_inc(S["gp_c0"], 1)
            nc.gpsimd.affine_select(out=ident[:], in_=ident[:], compare_op=ALU.not_equal, fill=1.0, base=0,
                                    pattern=[[-1, P]], channel_multiplier=1).then_inc(S["gp_const"], 1)
            nc.gpsimd.affine_select(out=tri_f[:], in_=tri_f[:], compare_op=ALU.is_ge, fill=0.0, base=0,
                                    pattern=[[1, P]], channel_multiplier=-1).then_inc(S["gp_const"], 1)
            pool.wait_ge(S["gp_c0"], 10)
            nc.gpsimd.affine_select(out=sel_f[:], in_=sel_f[:], compare_op=ALU.not_equal, fill=1.0, base=-32,
                                    pattern=[[-1, E], [0, P]], channel_multiplier=1).then_inc(S["gp_const"], 1)
            pool.wait_ge(S["b_in"], 48)
            unit(None, 0, None, 0, None)
            unit(None, 1, 0, 1, None)
            unit(0, 0, 1, 2, None)
            with pool.Fori(1, GROUPS - 3, 2) as u:
                unit(u, 1, u + 1, u + 2, u - 1)
                unit(u + 1, 0, u + 2, u + 3, u)
            unit(GROUPS - 3, 1, GROUPS - 2, GROUPS - 1, GROUPS - 4)
            unit(GROUPS - 2, 0, GROUPS - 1, None, GROUPS - 3)
            unit(GROUPS - 1, 1, None, None, GROUPS - 2)
            weigh(GROUPS - 1, CH - 1)
            step(4, None, 0, None, None, GROUPS - 1)


def kernel(L0_attn_x, L0_attn_w_qkv, L0_attn_b_qkv, L0_attn_w_out, L0_attn_b_out, L0_ffn_router_kernel_DE,
           L0_ffn_kernel_gating_EDF, L0_ffn_kernel_up_EDF, L0_ffn_kernel_down_EFD):
    import numpy as np
    import concourse.bacc as bacc
    from concourse import mybir
    from concourse.bass_utils import run_bass_kernel_spmd as run

    arrays = {
        "x": L0_attn_x,
        "w_qkv_t": np.asarray(L0_attn_w_qkv).T,
        "b_qkv": L0_attn_b_qkv,
        "w_out_t": np.asarray(L0_attn_w_out).T,
        "b_out": L0_attn_b_out,
        "w_router": L0_ffn_router_kernel_DE,
        "w_gate": L0_ffn_kernel_gating_EDF,
        "w_up": L0_ffn_kernel_up_EDF,
        "w_down": L0_ffn_kernel_down_EFD,
    }
    arrays = {n: np.ascontiguousarray(a) for n, a in arrays.items()}
    nc = bacc.Bacc("TRN2", target_bir_lowering=False, num_devices=1)
    args = [nc.dram_tensor(n, a.shape, mybir.dt.from_np(a.dtype), kind="ExternalInput").ap()
            for n, a in arrays.items()]
    shape = arrays["x"].shape
    args.append(nc.dram_tensor("out", shape, mybir.dt.from_np(arrays["x"].dtype), kind="ExternalOutput").ap())
    attn_moe_kernel(nc, *args)
    r = run(nc, [arrays], core_ids=[0])
    return r.results[0]["out"]
```

```python
import concourse.bass as bass
from concourse import mybir
from contextlib import ExitStack

F32 = mybir.dt.float32
F32R = mybir.dt.float32r
I32 = mybir.dt.int32
U32 = mybir.dt.uint32
ALU = mybir.AluOpType
ACT = mybir.ActivationFunctionType
AX_X = mybir.AxisListType.X

P = 128
TILES = 4
GT = P * TILES
HEADS = 16
D = P // HEADS
HALF = P // 2 * D
EPS_NORM = 1e-6
EPS_LN = 1e-5
RSQRT_MAGIC = float(0x5F3759DF)


def wait(eng, sem, value):
    if isinstance(value, int) and value <= 0:
        return
    eng.wait_ge(sem, value)


def attn_moe_kernel(nc, x, w_qkv_t, b_qkv, w_out_t, b_out, w_router, w_gate, w_up, w_down, out):
    B, T, C = x.shape
    E, _, F = w_gate.shape
    FC = F // P
    CH = E * FC
    GROUPS = B * T // GT
    QK = 2 * C
    assert C == P and T == 2 * P and CH == 16 and E == 8 and GROUPS == 16

    x_g = x.rearrange("(g b) (j p) c -> g p (b j) c", g=GROUPS, p=P)
    out_g = out.rearrange("(g b) (j p) c -> g p (b j) c", g=GROUPS, p=P)

    with ExitStack() as ctx:
        def sb(name, shape, dt=F32):
            return ctx.enter_context(nc.sbuf_tensor(name, shape, dt))

        def bank(name):
            return ctx.enter_context(nc.psum_tensor(name, [P, GT], F32))

        def sem(name):
            return ctx.enter_context(nc.semaphore(name))

        ident = sb("ident", [P, P])
        tri_f = sb("tri_f", [P, P])
        ones_f = sb("ones_f", [P, P])
        tri = sb("tri", [P, P], F32R)
        ones = sb("ones", [P, P], F32R)
        sel_f = sb("sel_f", [64, E, P])
        sel = sb("sel", [64, E, P], F32R)
        eidx = sb("eidx", [P, TILES, E])
        b_out_bc = sb("b_out_bc", [P, C])
        c_eps = sb("c_eps", [P, TILES])
        c_mhalf = sb("c_mhalf", [P, TILES])
        c_3half = sb("c_3half", [P, TILES])
        bq_f = sb("bq_f", [64, 3 * C])
        bq = sb("bq", [64, 3 * C], F32R)

        wqkv_hi = sb("wqkv_hi", [P, 3 * C], F32R)
        wqkv_lo = sb("wqkv_lo", [P, 3 * C], F32R)
        wo_hi = sb("wo_hi", [P, C], F32R)
        wo_lo = sb("wo_lo", [P, C], F32R)
        wr_hi = sb("wr_hi", [P, E], F32R)
        wr_lo = sb("wr_lo", [P, E], F32R)
        wg_hi = sb("wg_hi", [P, E, F], F32R)
        wg_lo = sb("wg_lo", [P, E, F], F32R)
        wu_hi = sb("wu_hi", [P, E, F], F32R)
        wu_lo = sb("wu_lo", [P, E, F], F32R)
        wd_hi = sb("wd_hi", [P, CH, C], F32R)
        wd_lo = sb("wd_lo", [P, CH, C], F32R)
        stage = sb("stage", [P, 3, 2048])

        xin = sb("xin", [P, TILES, C])
        xb = sb("xb", [P, TILES, C])
        xT_hi = sb("xT_hi", [P, GT], F32R)
        xT_lo = sb("xT_lo", [P, GT], F32R)
        z = sb("z", [P, TILES, 3 * C])
        neg = sb("neg", [P, TILES, QK])
        qk = sb("qk", [P, TILES, QK])
        kk_hi = sb("kk_hi", [P, TILES, C], F32R)
        kk_lo = sb("kk_lo", [P, TILES, C], F32R)
        qn = sb("qn", [P, TILES, C])
        nrm = sb("nrm", [P, TILES * HEADS])
        nrm_e = sb("nrm_e", [P, TILES * HEADS])
        rnrm = sb("rnrm", [P, TILES * HEADS])
        qs = sb("qs", [P, TILES, C])
        pf = sb("pf", [P, 4, HALF])
        p_hi = sb("p_hi", [P, 4, HALF], F32R)
        p_lo = sb("p_lo", [P, 4, HALF], F32R)
        zz = sb("zz", [P, 2, HALF])
        ctxt = sb("ctxt", [P, TILES, C])
        cT_hi = sb("cT_hi", [P, GT], F32R)
        cT_lo = sb("cT_lo", [P, GT], F32R)
        r1 = sb("r1", [P, TILES, C])
        x1 = sb("x1", [P, 2, TILES, C])
        x1T_hi = sb("x1T_hi", [P, 2, GT], F32R)
        x1T_lo = sb("x1T_lo", [P, 2, GT], F32R)

        stats = [sb(f"stats{n}", [P, TILES, 6]) for n in range(2)]
        mv = [sb(f"mv{n}", [P, TILES, 2]) for n in range(2)]
        nh = [sb(f"nh{n}", [P, TILES]) for n in range(2)]
        nv = [sb(f"nv{n}", [P, TILES]) for n in range(2)]
        ny = [sb(f"ny{n}", [P, TILES]) for n in range(2)]
        na = [sb(f"na{n}", [P, TILES]) for n in range(2)]

        mx = sb("mx", [P, TILES])
        lg = sb("lg", [P, TILES, E])
        ex = sb("ex", [P, TILES, E])
        sm = sb("sm", [P, TILES])
        rs = sb("rs", [P, TILES])
        prob = sb("prob", [P, TILES, E])
        top = sb("top", [P, TILES, 8])
        topi = sb("topi", [P, TILES, 8], U32)
        topf = sb("topf", [P, TILES, 8])
        dlt = sb("dlt", [P, TILES])
        th = sb("th", [P, TILES])
        wk = sb("wk", [P, 2, TILES])
        oh = sb("oh", [P, 2, TILES, E])
        wf = sb("wf", [P, 3, TILES, E])
        wT = sb("wT", [64, 2, GT], F32R)

        wbc = sb("wbc", [P, 2, GT])
        s_act = stage[:, 1, 0:2 * GT].rearrange("p (n t) -> p n t", n=2)
        sw = stage[:, 1, 2 * GT:].rearrange("p (n t) -> p n t", n=2)
        hf = stage[:, 2, 0:2 * GT].rearrange("p (n t) -> p n t", n=2)
        yTs = stage[:, 2, 2 * GT:3 * GT]
        r2 = stage[:, 2, 3 * GT:].rearrange("p (j c) -> p j c", j=TILES)
        h_hi = sb("h_hi", [P, 4, GT], F32R)
        h_lo = sb("h_lo", [P, 4, GT], F32R)
        res = sb("res", [P, TILES, C])

        G = [bank("G0"), bank("G1")]
        U = [bank("U0"), bank("U1")]
        Y = bank("Y")
        C0 = bank("C0")
        C1 = bank("C1")
        M = bank("M")

        names = """w_in wgu_in wd_in b_in gp_c0 gp_const dv_ones dv_const w_hi w_lo wT0
            x_in x_T xT_hi_d xT_lo_d xb_d qkv_d z_d neg_d ex_d qk_d kk_hi_d kk_lo_d cumk_d qn_d nrm_d
            nrme_d rnrm_d qs_d prod_d p_hi_d p_lo_d cum_d zz_d ctx_d ctx_T cT_hi_d cT_lo_d proj_d res_d
            st1_d mv1_d rn1_d x1_d x1_T x1T_hi_d x1T_lo_d logit_d rmax_d lg_d rex_d rchain th_d w_T wT_hi_d
            wT_lo_d wb_d wbs_d g_d u_d silu_d sw_d h_d h_hi_d h_lo_d dn_d yT_d y_T res2_d st2_d mv2_d
            rn2_d out_d stored dve_past pool_past""".split()
        S = {n: sem(n) for n in names}
        block = ctx.enter_context(nc.Block())

        RCH = 20
        NEWTON = 15

        qkv_bank = [C1, C0, C1, C1]
        LAG = 3

        def cum_bank(hs):
            return C0 if hs % 2 == 0 else C1

        @block.sync
        def _(sp):
            sp.dma_start(stage[:, 0, 0:3 * C], w_qkv_t).then_inc(S["w_in"], 16)
            sp.dma_start(stage[:, 0, 512:512 + C], w_out_t).then_inc(S["w_in"], 16)
            sp.dma_start(stage[:, 0, 1024:1024 + E], w_router).then_inc(S["w_in"], 16)
            sp.wait_ge(S["gp_c0"], 1)
            sp.dma_start(bq_f[0:1, :], b_qkv.rearrange("(o n) -> o n", o=1)).then_inc(S["b_in"], 16)
            sp.dma_start(bq_f[32:33, :], b_qkv.rearrange("(o n) -> o n", o=1)).then_inc(S["b_in"], 16)
            sp.dma_start(b_out_bc[:], b_out.rearrange("(o n) -> o n", o=1).to_broadcast([P, C])).then_inc(S["b_in"], 16)

            def load(g):
                wait(sp, S["x_T"], g)
                wait(sp, S["xb_d"], g)
                sp.dma_start(xin[:], x_g[g]).then_inc(S["x_in"], 16)

            def store(g):
                sp.wait_ge(S["out_d"], (g + 1) * TILES)
                sp.dma_start(out_g[g], res[:]).then_inc(S["stored"], 16)

            load(0)
            sp.dma_start(stage[:, 1, :].rearrange("p (e f) -> p e f", e=E),
                         w_gate.rearrange("e c f -> c e f")).then_inc(S["wgu_in"], 16)
            sp.dma_start(stage[:, 2, :].rearrange("p (e f) -> p e f", e=E),
                         w_up.rearrange("e c f -> c e f")).then_inc(S["wgu_in"], 16)
            sp.wait_ge(S["w_lo"], 3)
            sp.dma_start(stage[:, 0, :].rearrange("p (k c) -> p k c", k=CH),
                         w_down.rearrange("e (k f) c -> f (e k) c", f=P)).then_inc(S["wd_in"], 16)
            for g in (1, 2, 3):
                load(g)
            store(0)
            with sp.Fori(2, GROUPS - 2) as u:
                load(u + 2)
                store(u - 1)
            for g in range(GROUPS - 3, GROUPS):
                store(g)
            sp.wait_ge(S["stored"], 16 * GROUPS)

        @block.tensor
        def _(pe):
            mm = nc.tensor.matmul

            def three(dst, a_hi, a_lo, b_hi, b_lo, start=True, stop=True):
                mm(dst, a_hi, b_hi, start=start, stop=False)
                mm(dst, a_hi, b_lo, start=False, stop=False)
                return mm(dst, a_lo, b_hi, start=False, stop=stop)

            def transpose_x(h):
                wait(pe, S["x_in"], 16 * (h + 1))
                wait(pe, S["zz_d"], 8 * h - 1)
                for j in range(TILES):
                    last = nc.tensor.transpose(C0[:, j * P:(j + 1) * P], xin[:, j, :], ident[:])
                last.then_inc(S["x_T"], 1)

            def project(h, j):
                if j == 0:
                    pe.wait_ge(S["xT_hi_d"], h + 1)
                    pe.wait_ge(S["xT_lo_d"], h + 1)
                    wait(pe, S["zz_d"], 8 * h)
                elif j > 1:
                    pe.wait_ge(S["z_d"], 4 * h + (1 if j == 2 else 3))
                dst = qkv_bank[j][:, 0:3 * C]
                cols = slice(j * P, (j + 1) * P)
                mm(dst, xT_hi[:, cols], wqkv_hi[:], start=True, stop=False)
                mm(dst, xT_hi[:, cols], wqkv_lo[:], start=False, stop=False)
                mm(dst, xT_lo[:, cols], wqkv_hi[:], start=False, stop=False)
                mm(dst, ones[0:64, :], bq[:], start=False, stop=True).then_inc(S["qkv_d"], 1)

            def cumulate_k(h, y, tail):
                pe.wait_ge(S["kk_hi_d"], h + 1)
                pe.wait_ge(S["kk_lo_d"], h + 1)
                if y is not None:
                    pe.wait_ge(S["res2_d"], y + 1)
                elif tail is not None:
                    pe.wait_ge(S["res_d"], tail + 1)
                else:
                    pe.wait_ge(S["z_d"], 4 * h + 2)
                mm(C0[:], tri[:], kk_hi[:].rearrange("p j c -> p (j c)"), start=True, stop=False)
                mm(C0[:], tri[:], kk_lo[:].rearrange("p j c -> p (j c)"), start=False, stop=False)
                second = C0[:].rearrange("p (b j c) -> p b j c", b=2, j=2)[:, :, 1, :]
                mm(second, ones[:], kk_hi[:].rearrange("p (b j) c -> p b j c", b=2)[:, :, 0, :],
                   start=False, stop=False)
                mm(second, ones[:], kk_lo[:].rearrange("p (b j) c -> p b j c", b=2)[:, :, 0, :],
                   start=False, stop=True).then_inc(S["cumk_d"], 1)

            def cumulate(h, hs, tail):
                pe.wait_ge(S["p_hi_d"], 8 * h + hs + 1)
                pe.wait_ge(S["p_lo_d"], 8 * h + hs + 1)
                if hs == 0:
                    pe.wait_ge(S["qn_d"], h + 1)
                elif hs == 1:
                    if tail is not None:
                        pe.wait_ge(S["lg_d"], tail + 1)
                    else:
                        pe.wait_ge(S["z_d"], 4 * h + 4)
                else:
                    pe.wait_ge(S["zz_d"], 8 * h + hs - 1)
                dst = cum_bank(hs)
                second = (hs // 2) % 2 == 1
                mm(dst[:], tri[:], p_hi[:, hs % 4, :], start=True, stop=False)
                last = mm(dst[:], tri[:], p_lo[:, hs % 4, :], start=False, stop=not second)
                if second:
                    mm(dst[:], ones[:], p_hi[:, (hs - 2) % 4, :], start=False, stop=False)
                    last = mm(dst[:], ones[:], p_lo[:, (hs - 2) % 4, :], start=False, stop=True)
                last.then_inc(S["cum_d"], 1)

            def transpose_ctx(t, head):
                if head is not None:
                    pe.wait_ge(S["z_d"], 4 * head + 2)
                pe.wait_ge(S["ctx_d"], 8 * (t + 1))
                for j in range(TILES):
                    last = nc.tensor.transpose(C0[:, j * P:(j + 1) * P], ctxt[:, j, :], ident[:])
                last.then_inc(S["ctx_T"], 1)

            def out_project(t):
                pe.wait_ge(S["cT_hi_d"], t + 1)
                pe.wait_ge(S["cT_lo_d"], t + 1)
                for j in range(TILES):
                    cols = slice(j * P, (j + 1) * P)
                    last = three(C0[:, cols], cT_hi[:, cols], cT_lo[:, cols], wo_hi[:], wo_lo[:])
                last.then_inc(S["proj_d"], 1)

            def transpose_x1(t, par, head):
                pe.wait_ge(S["x1_d"], TILES * (t + 1))
                if head is not None:
                    pe.wait_ge(S["z_d"], 4 * head + 4)
                else:
                    pe.wait_ge(S["zz_d"], 8 * t + 8)
                for j in range(TILES):
                    last = nc.tensor.transpose(C1[:, j * P:(j + 1) * P], x1[:, par, j, :], ident[:])
                last.then_inc(S["x1_T"], 1)

            def logits(t, par):
                pe.wait_ge(S["x1T_hi_d"], t + 1)
                pe.wait_ge(S["x1T_lo_d"], t + 1)
                for j in range(TILES):
                    cols = slice(j * P, (j + 1) * P)
                    last = three(C1[:, j * E:(j + 1) * E], x1T_hi[:, par, cols], x1T_lo[:, par, cols],
                                 wr_hi[:], wr_lo[:])
                last.then_inc(S["logit_d"], 1)

            def transpose_w(t, moe):
                pe.wait_ge(S["rchain"], RCH * (t + 1))
                if moe is not None:
                    pe.wait_ge(S["wbs_d"], E * (moe + 1))
                for j in range(TILES):
                    last = nc.tensor.transpose(M[0:E, j * P:(j + 1) * P], wf[:, 2, j, :], ident[:])
                last.then_inc(S["w_T"], 1)

            def transpose_y(y, tail):
                pe.wait_ge(S["yT_d"], y + 1)
                if tail is not None:
                    pe.wait_ge(S["res_d"], tail + 1)
                else:
                    wait(pe, S["res2_d"], y)
                for j in range(TILES):
                    last = nc.tensor.transpose(C0[:, j * P:(j + 1) * P], yTs[:, j * P:(j + 1) * P], ident[:])
                last.then_inc(S["y_T"], 1)

            def spread(m, par, e):
                if e == 0:
                    pe.wait_ge(S["wT_hi_d"], m + 1)
                    pe.wait_ge(S["wT_lo_d"], m + 1)
                wait(pe, S["wbs_d"], E * m + e)
                mm(M[:], sel[:, e, :], wT[:, par, :], start=True, stop=True).then_inc(S["wb_d"], 1)

            def gate_up(m, par, k):
                n = CH * m + k
                if k == 0:
                    pe.wait_ge(S["x1T_hi_d"], m + 1)
                    pe.wait_ge(S["x1T_lo_d"], m + 1)
                e, f = k // FC, slice(k % FC * P, (k % FC + 1) * P)
                wait(pe, S["silu_d"], n - 1)
                three(G[k % 2][:], wg_hi[:, e, f], wg_lo[:, e, f], x1T_hi[:, par, :],
                      x1T_lo[:, par, :]).then_inc(S["g_d"], 1)
                wait(pe, S["h_d"], n - 1)
                three(U[k % 2][:], wu_hi[:, e, f], wu_lo[:, e, f], x1T_hi[:, par, :],
                      x1T_lo[:, par, :]).then_inc(S["u_d"], 1)

            def down(m, k):
                n = CH * m + k
                pe.wait_ge(S["h_hi_d"], n + 1)
                pe.wait_ge(S["h_lo_d"], n + 1)
                if k == 0:
                    wait(pe, S["yT_d"], m)
                three(Y[:], wd_hi[:, k, :], wd_lo[:, k, :], h_hi[:, k % 4, :], h_lo[:, k % 4, :],
                      start=(k == 0), stop=(k == CH - 1)).then_inc(S["dn_d"], 1)

            def step(s, m, par, tail, head, y, nxt):
                if head is not None:
                    if s == 0:
                        project(head, 0)
                        project(head, 1)
                    if s == 1:
                        project(head, 2)
                    if s == 2:
                        project(head, 3)
                if s == 1 and tail is not None:
                    transpose_ctx(tail, head)
                if s == 2 and tail is not None:
                    out_project(tail)
                if s == 4 and y is not None:
                    transpose_y(y, tail)
                if s == 6 and head is not None:
                    cumulate_k(head, y, tail)
                if s == 6 and tail is not None:
                    transpose_x1(tail, 1 - par, head)
                if s == 7 and tail is not None:
                    logits(tail, 1 - par)
                if 8 <= s <= 15 and head is not None:
                    cumulate(head, s - 8, tail)
                if s == 14 and tail is not None:
                    transpose_w(tail, m)
                if s == 15 and nxt is not None:
                    transpose_x(nxt)

            def unit(m, par, tail, head, y, nxt):
                for s in range(CH):
                    if m is not None:
                        if s % FC == 0:
                            spread(m, par, s // FC)
                        gate_up(m, par, s)
                        if s >= LAG:
                            down(m, s - LAG)
                        elif y is not None:
                            down(y, CH - LAG + s)
                    step(s, m, par, tail, head, y, nxt)

            pe.wait_ge(S["gp_const"], 3)
            pe.wait_ge(S["dv_const"], 3)
            pe.wait_ge(S["w_hi"], 4)
            pe.wait_ge(S["w_lo"], 4)
            transpose_x(0)
            unit(None, 0, None, 0, None, 1)
            unit(None, 1, 0, 1, None, 2)
            pe.wait_ge(S["wT0"], 1)
            pe.wait_ge(S["w_hi"], 7)
            pe.wait_ge(S["w_lo"], 7)
            unit(0, 0, 1, 2, None, 3)
            with pe.Fori(1, GROUPS - 3, 2) as u:
                unit(u, 1, u + 1, u + 2, u - 1, u + 3)
                unit(u + 1, 0, u + 2, u + 3, u, u + 4)
            unit(GROUPS - 3, 1, GROUPS - 2, GROUPS - 1, GROUPS - 4, None)
            unit(GROUPS - 2, 0, GROUPS - 1, None, GROUPS - 3, None)
            unit(GROUPS - 1, 1, None, None, GROUPS - 2, None)
            for k in range(CH - LAG, CH):
                down(GROUPS - 1, k)
            transpose_y(GROUPS - 1, None)

        @block.scalar
        def _(act):
            def copy(dst, src):
                return nc.scalar.activation(dst, src, ACT.Copy)

            def z_copy(h, j):
                act.wait_ge(S["qkv_d"], 4 * h + j + 1)
                if j == 0:
                    wait(act, S["qk_d"], h)
                    wait(act, S["prod_d"], 8 * h)
                copy(z[:, j, :], qkv_bank[j][:, 0:3 * C]).then_inc(S["z_d"], 1)

            def product_hi(h, hs):
                act.wait_ge(S["prod_d"], 8 * h + hs + 1)
                wait(act, S["cum_d"], 8 * h + hs - (1 if hs // 2 % 2 == 0 else 3))
                copy(p_hi[:, hs % 4, :], pf[:, hs % 4, :]).then_inc(S["p_hi_d"], 1)

            def silu(m, k):
                n = CH * m + k
                act.wait_ge(S["g_d"], n + 1)
                wait(act, S["sw_d"], n - 1)
                nc.scalar.activation(s_act[:, k % 2, :], G[k % 2][:], ACT.Silu).then_inc(S["silu_d"], 1)

            def hidden_hi(m, k):
                n = CH * m + k
                act.wait_ge(S["h_d"], n + 1)
                wait(act, S["dn_d"], n - 3)
                copy(h_hi[:, k % 4, :], hf[:, k % 2, :]).then_inc(S["h_hi_d"], 1)

            def weights_out(m, e):
                act.wait_ge(S["wb_d"], E * m + e + 1)
                wait(act, S["sw_d"], CH * m + FC * (e - 1))
                copy(wbc[:, e % 2, :], M[:]).then_inc(S["wbs_d"], 1)

            def x_hi(h):
                act.wait_ge(S["x_T"], h + 1)
                wait(act, S["qkv_d"], 4 * h)
                copy(xT_hi[:], C0[:]).then_inc(S["xT_hi_d"], 1)

            def step(s, m, par, tail, head, y, nxt):
                if head is not None:
                    if s == 0:
                        z_copy(head, 0)
                        z_copy(head, 1)
                    if s == 1:
                        z_copy(head, 2)
                    if s == 2:
                        z_copy(head, 3)
                if s == 1 and tail is not None:
                    act.wait_ge(S["ctx_T"], tail + 1)
                    wait(act, S["proj_d"], tail)
                    copy(cT_hi[:], C0[:]).then_inc(S["cT_hi_d"], 1)
                if s == 3 and y is not None:
                    act.wait_ge(S["dn_d"], CH * (y + 1))
                    wait(act, S["y_T"], y)
                    copy(yTs, Y[:]).then_inc(S["yT_d"], 1)
                if s == 3 and head is not None:
                    act.wait_ge(S["neg_d"], head + 1)
                    nc.scalar.activation(neg[:], neg[:], ACT.Exp).then_inc(S["ex_d"], 1)
                if s == 4 and head is not None:
                    act.wait_ge(S["qk_d"], head + 1)
                    wait(act, S["cumk_d"], head)
                    copy(kk_hi[:], qk[:, :, C:QK]).then_inc(S["kk_hi_d"], 1)
                if s == 6 and tail is not None:
                    act.wait_ge(S["x1_T"], tail + 1)
                    if not isinstance(tail, int) or tail >= 2:
                        act.wait_ge(S["u_d"], CH * (tail - 1))
                        act.wait_ge(S["logit_d"], tail)
                    copy(x1T_hi[:, 1 - par, :], C1[:]).then_inc(S["x1T_hi_d"], 1)
                if s == 8 and tail is not None:
                    act.wait_ge(S["lg_d"], tail + 1)
                    wait(act, S["rchain"], RCH * tail)
                    nc.scalar.activation(ex[:], lg[:], ACT.Exp).then_inc(S["rex_d"], 1)
                if 6 <= s <= 13 and head is not None:
                    product_hi(head, s - 6)
                if s == 11 and tail is not None:
                    act.wait_ge(S["rchain"], RCH * tail + 12)
                    nc.scalar.activation(th[:], dlt[:], ACT.Tanh, scale=0.5).then_inc(S["th_d"], 1)
                if s == 14 and tail is not None:
                    act.wait_ge(S["w_T"], tail + 1)
                    wait(act, S["wb_d"], E * (tail - 1))
                    copy(wT[0:E, 1 - par, :], M[0:E, :]).then_inc(S["wT_hi_d"], 1)
                if s == 15 and nxt is not None:
                    x_hi(nxt)

            def unit(m, par, tail, head, y, nxt):
                for s in range(CH):
                    if m is not None:
                        if s % FC == 0:
                            weights_out(m, s // FC)
                        silu(m, s)
                        if s >= 1:
                            hidden_hi(m, s - 1)
                        elif y is not None:
                            hidden_hi(y, CH - 1)
                    step(s, m, par, tail, head, y, nxt)

            act.wait_ge(S["w_in"], 48)
            copy(wqkv_hi[:], stage[:, 0, 0:3 * C]).then_inc(S["w_hi"], 1)
            copy(wo_hi[:], stage[:, 0, 512:512 + C]).then_inc(S["w_hi"], 1)
            copy(wr_hi[:], stage[:, 0, 1024:1024 + E]).then_inc(S["w_hi"], 1)
            act.wait_ge(S["b_in"], 48)
            copy(bq[0:32, :], bq_f[0:32, :]).then_inc(S["w_hi"], 1)
            x_hi(0)
            unit(None, 0, None, 0, None, 1)
            act.wait_ge(S["wgu_in"], 32)
            act.wait_ge(S["wd_in"], 16)
            copy(wg_hi[:].rearrange("p e f -> p (e f)"), stage[:, 1, :]).then_inc(S["w_hi"], 1)
            copy(wu_hi[:].rearrange("p e f -> p (e f)"), stage[:, 2, :]).then_inc(S["w_hi"], 1)
            copy(wd_hi[:].rearrange("p k c -> p (k c)"), stage[:, 0, :]).then_inc(S["w_hi"], 1)
            unit(None, 1, 0, 1, None, 2)
            unit(0, 0, 1, 2, None, 3)
            with act.Fori(1, GROUPS - 3, 2) as u:
                unit(u, 1, u + 1, u + 2, u - 1, u + 3)
                unit(u + 1, 0, u + 2, u + 3, u, u + 4)
            unit(GROUPS - 3, 1, GROUPS - 2, GROUPS - 1, GROUPS - 4, None)
            unit(GROUPS - 2, 0, GROUPS - 1, None, GROUPS - 3, None)
            unit(GROUPS - 1, 1, None, None, GROUPS - 2, None)
            hidden_hi(GROUPS - 1, CH - 1)
            act.wait_ge(S["dn_d"], CH * GROUPS)
            act.wait_ge(S["y_T"], GROUPS - 1)
            copy(yTs, Y[:]).then_inc(S["yT_d"], 1)

        @block.vector
        def _(dve):
            tt = nc.vector.tensor_tensor
            ts = nc.vector.tensor_scalar

            def low(dst, src, hi):
                return tt(dst, src, hi.bitcast(F32), ALU.subtract)

            def hidden(m, k):
                n = CH * m + k
                dve.wait_ge(S["sw_d"], n + 1)
                dve.wait_ge(S["u_d"], n + 1)
                wait(dve, S["h_hi_d"], n - 1)
                wait(dve, S["h_lo_d"], n - 1)
                tt(hf[:, k % 2, :], U[k % 2][:], sw[:, k % 2, :], ALU.mult).then_inc(S["h_d"], 1)

            def hidden_lo(m, k):
                n = CH * m + k
                dve.wait_ge(S["h_hi_d"], n + 1)
                wait(dve, S["dn_d"], n - 3)
                low(h_lo[:, k % 4, :], hf[:, k % 2, :], h_hi[:, k % 4, :]).then_inc(S["h_lo_d"], 1)

            def statistics(n, g, src):
                st, mvs = S[f"st{n + 1}_d"], S[f"mv{n + 1}_d"]
                wait(dve, mvs, TILES * g)
                for j in range(TILES):
                    nc.vector.bn_stats(stats[n][:, j, :], src[:, j, :]).then_inc(st, 1)
                wait(dve, S["x1_d"] if n == 0 else S["out_d"], TILES * g)
                dve.wait_ge(st, TILES * (g + 1))
                dve.sem_inc(S["dve_past"], 1)
                for j in range(TILES):
                    nc.vector.bn_aggr(mv[n][:, j, :], stats[n][:, j, :]).then_inc(mvs, 1)

            def half_product_lo(h, hs):
                dve.wait_ge(S["p_hi_d"], 8 * h + hs + 1)
                wait(dve, S["cum_d"], 8 * h + hs - (1 if hs // 2 % 2 == 0 else 3))
                low(p_lo[:, hs % 4, :], pf[:, hs % 4, :], p_hi[:, hs % 4, :]).then_inc(S["p_lo_d"], 1)

            def apply_q(h, hs):
                j, half = hs // 2, hs % 2
                dve.wait_ge(S["cum_d"], 8 * h + hs + 1)
                dve.wait_ge(S["qs_d"], h + 1)
                wait(dve, S["ctx_d"], 8 * h + hs - 1)
                q4 = qs[:, j, half * 64:(half + 1) * 64].rearrange("p (h o d) -> p h o d", o=1, d=D)
                tt(zz[:, hs % 2, :].rearrange("p (h e d) -> p h e d", e=D, d=D),
                   cum_bank(hs)[:].rearrange("p (h e d) -> p h e d", e=D, d=D),
                   q4.to_broadcast([P, HEADS // 2, D, D]), ALU.mult).then_inc(S["zz_d"], 1)

            def contract(h, hs):
                j, half = hs // 2, hs % 2
                dve.wait_ge(S["zz_d"], 8 * h + hs + 1)
                wait(dve, S["ctx_T"], h)
                nc.vector.tensor_reduce(ctxt[:, j, half * 64:(half + 1) * 64],
                                        zz[:, hs % 2, :].rearrange("p (c d) -> p c d", d=D),
                                        AX_X, ALU.add).then_inc(S["ctx_d"], 1)

            def bc(v):
                return v.rearrange("p (j o) -> p j o", o=1).to_broadcast([P, TILES, E])

            def router(t, a, b):
                base = RCH * t
                c = S["rchain"]

                def after(n):
                    wait(dve, c, base + n)
                done = 0
                def s1():
                    dve.wait_ge(S["rex_d"], t + 1)
                    return nc.vector.tensor_reduce(sm[:], ex[:], AX_X, ALU.add)
                def s2():
                    after(1)
                    return nc.vector.reciprocal(rs[:], sm[:])
                def s3():
                    after(2)
                    return tt(prob[:], ex[:], bc(rs[:]), ALU.mult)
                def s_max(j):
                    def s():
                        if j == 0:
                            after(3)
                            dve.sem_inc(S["dve_past"], 1)
                        return nc.vector.max(top[:, j, :], prob[:, j, :])
                    return s
                def s_idx(j):
                    def s():
                        if j == 0:
                            after(7)
                            dve.sem_inc(S["dve_past"], 1)
                        return nc.vector.max_index(topi[:, j, :], top[:, j, :], prob[:, j, :])
                    return s
                def s12():
                    after(7)
                    wait(dve, S["th_d"], t)
                    return tt(dlt[:], top[:, :, 0], top[:, :, 1], ALU.subtract)
                def s13():
                    after(11)
                    return nc.vector.tensor_copy(topf[:], topi[:])
                def s14():
                    dve.wait_ge(S["th_d"], t + 1)
                    return ts(wk[:, 0, :], th[:], 0.5, 0.5, ALU.mult, ALU.add)
                def s15():
                    return ts(wk[:, 1, :], th[:], -0.5, 0.5, ALU.mult, ALU.add)
                def s_oh(n):
                    def s():
                        after(13)
                        return tt(oh[:, n], eidx[:], bc(topf[:, :, n]), ALU.is_equal)
                    return s
                def s_w(n):
                    def s():
                        after(16 + n)
                        return tt(wf[:, n], oh[:, n], bc(wk[:, n, :]), ALU.mult)
                    return s
                def s20():
                    after(19)
                    wait(dve, S["w_T"], t)
                    return tt(wf[:, 2], wf[:, 0], wf[:, 1], ALU.add)
                steps = ([s1, s2, s3] + [s_max(j) for j in range(TILES)] + [s_idx(j) for j in range(TILES)]
                         + [s12, s13, s14, s15, s_oh(0), s_oh(1), s_w(0), s_w(1), s20])
                for n in range(a, b + 1):
                    steps[n - 1]().then_inc(c, 1)

            def x_lo(h):
                dve.wait_ge(S["xT_hi_d"], h + 1)
                wait(dve, S["qkv_d"], 4 * h)
                low(xT_lo[:], C0[:], xT_hi[:]).then_inc(S["xT_lo_d"], 1)

            def residual_1(t):
                dve.wait_ge(S["proj_d"], t + 1)
                dve.wait_ge(S["xb_d"], t + 1)
                wait(dve, S["x1_d"], TILES * t)
                tt(r1[:].rearrange("p j c -> p (j c)"), C0[:], xb[:].rearrange("p j c -> p (j c)"),
                   ALU.add).then_inc(S["res_d"], 1)
                dve.wait_ge(S["res_d"], t + 1)
                statistics(0, t, r1)

            def residual_2(y, par):
                dve.wait_ge(S["y_T"], y + 1)
                wait(dve, S["out_d"], TILES * y)
                tt(r2.rearrange("p j c -> p (j c)"), C0[:],
                   x1[:, par, :, :].rearrange("p j c -> p (j c)"), ALU.add).then_inc(S["res2_d"], 1)
                dve.wait_ge(S["res2_d"], y + 1)
                statistics(1, y, r2)

            def normalize(n, g, src, dst):
                dve.wait_ge(S[f"rn{n + 1}_d"], NEWTON * (g + 1))
                for j in range(TILES):
                    ts(dst[:, j, :], src[:, j, :], mv[n][:, j, 0:1], ny[n][:, j:j + 1], ALU.subtract,
                       ALU.mult).then_inc(S["x1_d"] if n == 0 else S["out_d"], 1)

            def norm(h):
                dve.wait_ge(S["cumk_d"], h + 1)
                wait(dve, S["nrm_d"], h)
                tt(qn[:], C0[:].rearrange("p (j c) -> p j c", c=C), qk[:, :, 0:C], ALU.mult).then_inc(S["qn_d"], 1)
                dve.wait_ge(S["qn_d"], h + 1)
                nc.vector.tensor_reduce(nrm[:], qn[:].rearrange("p j (h d) -> p (j h) d", d=D),
                                        AX_X, ALU.add).then_inc(S["nrm_d"], 1)
                dve.wait_ge(S["nrm_d"], h + 1)
                ts(nrm_e[:], nrm[:], EPS_NORM, None, ALU.add).then_inc(S["nrme_d"], 1)
                dve.wait_ge(S["nrme_d"], h + 1)
                nc.vector.reciprocal(rnrm[:], nrm_e[:]).then_inc(S["rnrm_d"], 1)
                dve.wait_ge(S["rnrm_d"], h + 1)
                wait(dve, S["zz_d"], 8 * h)
                tt(qs[:].rearrange("p j (h d) -> p j h d", d=D),
                   qk[:, :, 0:C].rearrange("p j (h d) -> p j h d", d=D),
                   rnrm[:].rearrange("p (j h o) -> p j h o", o=1, h=HEADS).to_broadcast([P, TILES, HEADS, D]),
                   ALU.mult).then_inc(S["qs_d"], 1)

            def early(s, m, par, tail, head, y, nxt):
                if 9 <= s <= 15 and head is not None:
                    apply_q(head, s - 9)
                    contract(head, s - 9)
                if s == 0 and tail is not None:
                    apply_q(tail, 7)
                    contract(tail, 7)
                if s == 3 and tail is not None:
                    residual_1(tail)
                if s == 3 and head is not None:
                    dve.wait_ge(S["z_d"], 4 * head + 4)
                    wait(dve, S["qk_d"], head)
                    ts(neg[:], z[:, :, 0:QK], 0.0, None, ALU.min).then_inc(S["neg_d"], 1)
                if s == 5 and y is not None:
                    residual_2(y, 1 - par)
                if s == 5 and head is not None:
                    dve.wait_ge(S["kk_hi_d"], head + 1)
                    wait(dve, S["cumk_d"], head)
                    low(kk_lo[:], qk[:, :, C:QK], kk_hi[:]).then_inc(S["kk_lo_d"], 1)
                if s == 6 and tail is not None:
                    wait(dve, S["x1_T"], tail - 1)
                    if not isinstance(tail, int) or tail >= 2:
                        dve.wait_ge(S["res2_d"], tail - 1)
                    normalize(0, tail, r1, x1[:, 1 - par])
                if s == 15 and y is not None:
                    wait(dve, S["stored"], 16 * y)
                    normalize(1, y, r2, res)
                if s == 7 and head is not None:
                    norm(head)
                if 7 <= s <= 14 and head is not None:
                    half_product_lo(head, s - 7)
                if s == 8 and tail is not None:
                    dve.wait_ge(S["logit_d"], tail + 1)
                    lg3 = C1[:, 0:TILES * E].rearrange("p (j e) -> p j e", e=E)
                    wait(dve, S["lg_d"], tail)
                    nc.vector.tensor_reduce(mx[:], lg3, AX_X, ALU.max).then_inc(S["rmax_d"], 1)
                    dve.wait_ge(S["rmax_d"], tail + 1)
                    wait(dve, S["rex_d"], tail)
                    tt(lg[:], lg3, bc(mx[:]), ALU.subtract).then_inc(S["lg_d"], 1)
                if tail is not None and s in (9, 10, 11, 12, 13):
                    router(tail, *{9: (1, 3), 10: (4, 11), 11: (12, 13), 12: (14, 17), 13: (18, 20)}[s])

            def late(s, m, par, tail, head, y, nxt):
                if s == 1 and tail is not None:
                    dve.wait_ge(S["cT_hi_d"], tail + 1)
                    wait(dve, S["proj_d"], tail)
                    low(cT_lo[:], C0[:], cT_hi[:]).then_inc(S["cT_lo_d"], 1)
                if s == 3 and head is not None:
                    dve.wait_ge(S["ex_d"], head + 1)
                    wait(dve, S["qs_d"], head)
                    wait(dve, S["kk_lo_d"], head)
                    wait(dve, S["kk_hi_d"], head)
                    wait(dve, S["prod_d"], 8 * head)
                    nc.vector.scalar_tensor_tensor(out=qk[:], in0=z[:, :, 0:QK], scalar=0.0, in1=neg[:],
                                                   op0=ALU.max, op1=ALU.add).then_inc(S["qk_d"], 1)
                if s == 6 and tail is not None:
                    dve.wait_ge(S["x1T_hi_d"], tail + 1)
                    if not isinstance(tail, int) or tail >= 2:
                        dve.wait_ge(S["u_d"], CH * (tail - 1))
                        dve.wait_ge(S["logit_d"], tail)
                    low(x1T_lo[:, 1 - par, :], C1[:], x1T_hi[:, 1 - par, :]).then_inc(S["x1T_lo_d"], 1)
                if s == 14 and tail is not None:
                    dve.wait_ge(S["wT_hi_d"], tail + 1)
                    wait(dve, S["wb_d"], E * (tail - 1))
                    low(wT[32:32 + E, 1 - par, :], M[0:E, :], wT[0:E, 1 - par, :]).then_inc(S["wT_lo_d"], 1)
                if s == 15 and nxt is not None:
                    x_lo(nxt)

            def unit(m, par, tail, head, y, nxt):
                for s in range(CH):
                    if m is not None:
                        if s >= 1:
                            hidden(m, s - 1)
                        elif y is not None:
                            hidden(y, CH - 1)
                    early(s, m, par, tail, head, y, nxt)
                    if m is not None:
                        if s >= 1:
                            hidden_lo(m, s - 1)
                        elif y is not None:
                            hidden_lo(y, CH - 1)
                    late(s, m, par, tail, head, y, nxt)

            dve.wait_ge(S["gp_const"], 3)
            nc.vector.tensor_copy(tri[:], tri_f[:]).then_inc(S["dv_const"], 1)
            nc.vector.tensor_copy(ones[:], ones_f[:]).then_inc(S["dv_const"], 1)
            nc.vector.tensor_copy(sel[:].rearrange("p e c -> p (e c)"),
                                  sel_f[:].rearrange("p e c -> p (e c)")).then_inc(S["dv_const"], 1)
            nc.vector.memset(wT[:].bitcast(F32), 0.0).then_inc(S["wT0"], 1)
            dve.wait_ge(S["wT0"], 1)
            dve.wait_ge(S["w_hi"], 4)
            low(wqkv_lo[:], stage[:, 0, 0:3 * C], wqkv_hi[:]).then_inc(S["w_lo"], 1)
            low(wo_lo[:], stage[:, 0, 512:512 + C], wo_hi[:]).then_inc(S["w_lo"], 1)
            low(wr_lo[:], stage[:, 0, 1024:1024 + E], wr_hi[:]).then_inc(S["w_lo"], 1)
            low(bq[32:64, :], bq_f[0:32, :], bq[0:32, :]).then_inc(S["w_lo"], 1)
            x_lo(0)
            unit(None, 0, None, 0, None, 1)
            dve.wait_ge(S["w_hi"], 7)
            low(wg_lo[:].rearrange("p e f -> p (e f)"), stage[:, 1, :],
                wg_hi[:].rearrange("p e f -> p (e f)")).then_inc(S["w_lo"], 1)
            low(wu_lo[:].rearrange("p e f -> p (e f)"), stage[:, 2, :],
                wu_hi[:].rearrange("p e f -> p (e f)")).then_inc(S["w_lo"], 1)
            low(wd_lo[:].rearrange("p k c -> p (k c)"), stage[:, 0, :],
                wd_hi[:].rearrange("p k c -> p (k c)")).then_inc(S["w_lo"], 1)
            unit(None, 1, 0, 1, None, 2)
            unit(0, 0, 1, 2, None, 3)
            with dve.Fori(1, GROUPS - 3, 2) as u:
                unit(u, 1, u + 1, u + 2, u - 1, u + 3)
                unit(u + 1, 0, u + 2, u + 3, u, u + 4)
            unit(GROUPS - 3, 1, GROUPS - 2, GROUPS - 1, GROUPS - 4, None)
            unit(GROUPS - 2, 0, GROUPS - 1, None, GROUPS - 3, None)
            unit(GROUPS - 1, 1, None, None, GROUPS - 2, None)
            hidden(GROUPS - 1, CH - 1)
            hidden_lo(GROUPS - 1, CH - 1)
            residual_2(GROUPS - 1, 1)
            dve.wait_ge(S["stored"], 16 * (GROUPS - 1))
            normalize(1, GROUPS - 1, r2, res)

        @block.gpsimd
        def _(pool):
            gtt = nc.gpsimd.tensor_tensor
            gts = nc.gpsimd.tensor_scalar

            def weigh(m, k):
                n = CH * m + k
                pool.wait_ge(S["silu_d"], n + 1)
                pool.wait_ge(S["wbs_d"], E * m + k // FC + 1)
                wait(pool, S["h_d"], n - 1)
                gtt(sw[:, k % 2, :], s_act[:, k % 2, :], wbc[:, (k // FC) % 2, :], ALU.mult).then_inc(S["sw_d"], 1)

            def half_product(h, hs):
                j, half = hs // 2, hs % 2
                if hs == 0:
                    pool.wait_ge(S["qk_d"], h + 1)
                wait(pool, S["p_hi_d"], 8 * h + hs - 3)
                wait(pool, S["p_lo_d"], 8 * h + hs - 3)
                k0, v0 = C + half * 64, QK + half * 64
                k4 = qk[:, j, k0:k0 + 64].rearrange("p (h o d) -> p h o d", o=1, d=D)
                v4 = z[:, j, v0:v0 + 64].rearrange("p (h e o) -> p h e o", o=1, e=D)
                shape = [P, HEADS // 2, D, D]
                gtt(pf[:, hs % 4, :].rearrange("p (h e d) -> p h e d", e=D, d=D), k4.to_broadcast(shape),
                    v4.to_broadcast(shape), ALU.mult).then_inc(S["prod_d"], 1)

            def rsqrt(n, g, part):
                c = S[f"rn{n + 1}_d"]
                v, vh, y, a = nv[n][:], nh[n][:], ny[n][:], na[n][:]
                base = NEWTON * g
                if part == 0:
                    pool.wait_ge(S[f"mv{n + 1}_d"], TILES * (g + 1))
                    wait(pool, S["x1_d"] if n == 0 else S["out_d"], TILES * g)
                    gtt(v, mv[n][:, :, 1], c_eps[:], ALU.add).then_inc(c, 1)
                    pool.wait_ge(c, base + 1)
                    gtt(vh, v, c_mhalf[:], ALU.mult).then_inc(c, 1)
                    gts(y.bitcast(I32), v.bitcast(I32), -0.5, RSQRT_MAGIC, ALU.mult, ALU.add).then_inc(c, 1)
                for n in ((0,), (1, 2))[part]:
                    at = 3 + 4 * n
                    pool.wait_ge(c, base + at)
                    gtt(a, y, y, ALU.mult).then_inc(c, 1)
                    pool.wait_ge(c, base + at + 1)
                    gtt(a, a, vh, ALU.mult).then_inc(c, 1)
                    pool.wait_ge(c, base + at + 2)
                    gtt(a, a, c_3half[:], ALU.add).then_inc(c, 1)
                    pool.wait_ge(c, base + at + 3)
                    gtt(y, y, a, ALU.mult).then_inc(c, 1)

            def step(s, m, par, tail, head, y, nxt):
                if s == 3 and head is not None:
                    pool.wait_ge(S["x_in"], 16 * (head + 1))
                    wait(pool, S["res_d"], head)
                    gtt(xb[:], xin[:], b_out_bc[:].rearrange("p (o c) -> p o c", o=1)
                        .to_broadcast([P, TILES, C]), ALU.add).then_inc(S["xb_d"], 1)
                if 5 <= s <= 12 and head is not None:
                    half_product(head, s - 5)
                if s == 4 and tail is not None:
                    rsqrt(0, tail, 0)
                if s == 5 and tail is not None:
                    rsqrt(0, tail, 1)
                if s == 13 and y is not None:
                    rsqrt(1, y, 0)
                if s == 14 and y is not None:
                    rsqrt(1, y, 1)

            def unit(m, par, tail, head, y, nxt):
                for s in range(CH):
                    if m is not None:
                        if s >= 1:
                            weigh(m, s - 1)
                        elif y is not None:
                            weigh(y, CH - 1)
                    step(s, m, par, tail, head, y, nxt)

            nc.gpsimd.memset(bq_f[:], 0.0).then_inc(S["gp_c0"], 1)
            nc.gpsimd.memset(ident[:], 0.0).then_inc(S["gp_c0"], 1)
            nc.gpsimd.memset(tri_f[:], 1.0).then_inc(S["gp_c0"], 1)
            nc.gpsimd.memset(sel_f[:], 0.0).then_inc(S["gp_c0"], 1)
            nc.gpsimd.memset(ones_f[:], 1.0).then_inc(S["gp_c0"], 1)
            nc.gpsimd.iota(eidx[:], pattern=[[0, TILES], [1, E]], base=0, channel_multiplier=0,
                           allow_small_or_imprecise_dtypes=True).then_inc(S["gp_c0"], 1)
            nc.gpsimd.memset(c_eps[:], EPS_LN).then_inc(S["gp_c0"], 1)
            nc.gpsimd.memset(c_mhalf[:], -0.5).then_inc(S["gp_c0"], 1)
            nc.gpsimd.memset(c_3half[:], 1.5).then_inc(S["gp_c0"], 1)
            pool.wait_ge(S["gp_c0"], 9)
            nc.gpsimd.affine_select(out=sel_f[:], in_=sel_f[:], compare_op=ALU.not_equal, fill=1.0, base=0,
                                    pattern=[[-1, E], [0, P]], channel_multiplier=1).then_inc(S["gp_c0"], 1)
            nc.gpsimd.affine_select(out=ident[:], in_=ident[:], compare_op=ALU.not_equal, fill=1.0, base=0,
                                    pattern=[[-1, P]], channel_multiplier=1).then_inc(S["gp_const"], 1)
            nc.gpsimd.affine_select(out=tri_f[:], in_=tri_f[:], compare_op=ALU.is_ge, fill=0.0, base=0,
                                    pattern=[[1, P]], channel_multiplier=-1).then_inc(S["gp_const"], 1)
            pool.wait_ge(S["gp_c0"], 10)
            nc.gpsimd.affine_select(out=sel_f[:], in_=sel_f[:], compare_op=ALU.not_equal, fill=1.0, base=-32,
                                    pattern=[[-1, E], [0, P]], channel_multiplier=1).then_inc(S["gp_const"], 1)
            pool.wait_ge(S["b_in"], 48)
            unit(None, 0, None, 0, None, 1)
            unit(None, 1, 0, 1, None, 2)
            unit(0, 0, 1, 2, None, 3)
            with pool.Fori(1, GROUPS - 3, 2) as u:
                unit(u, 1, u + 1, u + 2, u - 1, u + 3)
                unit(u + 1, 0, u + 2, u + 3, u, u + 4)
            unit(GROUPS - 3, 1, GROUPS - 2, GROUPS - 1, GROUPS - 4, None)
            unit(GROUPS - 2, 0, GROUPS - 1, None, GROUPS - 3, None)
            unit(GROUPS - 1, 1, None, None, GROUPS - 2, None)
            weigh(GROUPS - 1, CH - 1)
            rsqrt(1, GROUPS - 1, 0)
            rsqrt(1, GROUPS - 1, 1)


def kernel(L0_attn_x, L0_attn_w_qkv, L0_attn_b_qkv, L0_attn_w_out, L0_attn_b_out, L0_ffn_router_kernel_DE,
           L0_ffn_kernel_gating_EDF, L0_ffn_kernel_up_EDF, L0_ffn_kernel_down_EFD):
    import numpy as np
    import concourse.bacc as bacc
    from concourse import mybir
    from concourse.bass_utils import run_bass_kernel_spmd as run

    arrays = {
        "x": L0_attn_x,
        "w_qkv_t": np.asarray(L0_attn_w_qkv).T,
        "b_qkv": L0_attn_b_qkv,
        "w_out_t": np.asarray(L0_attn_w_out).T,
        "b_out": L0_attn_b_out,
        "w_router": L0_ffn_router_kernel_DE,
        "w_gate": L0_ffn_kernel_gating_EDF,
        "w_up": L0_ffn_kernel_up_EDF,
        "w_down": L0_ffn_kernel_down_EFD,
    }
    arrays = {n: np.ascontiguousarray(a) for n, a in arrays.items()}
    nc = bacc.Bacc("TRN2", target_bir_lowering=False, num_devices=1)
    args = [nc.dram_tensor(n, a.shape, mybir.dt.from_np(a.dtype), kind="ExternalInput").ap()
            for n, a in arrays.items()]
    shape = arrays["x"].shape
    args.append(nc.dram_tensor("out", shape, mybir.dt.from_np(arrays["x"].dtype), kind="ExternalOutput").ap())
    attn_moe_kernel(nc, *args)
    r = run(nc, [arrays], core_ids=[0])
    return r.results[0]["out"]
```

```python
import concourse.bass as bass
from concourse import mybir
from contextlib import ExitStack

F32 = mybir.dt.float32
F32R = mybir.dt.float32r
I32 = mybir.dt.int32
U32 = mybir.dt.uint32
ALU = mybir.AluOpType
ACT = mybir.ActivationFunctionType
AX_X = mybir.AxisListType.X

P = 128
TILES = 4
GT = P * TILES
HEADS = 16
D = P // HEADS
HALF = P // 2 * D
EPS_NORM = 1e-6
EPS_LN = 1e-5
RSQRT_MAGIC = float(0x5F3759DF)


def wait(eng, sem, value):
    if isinstance(value, int) and value <= 0:
        return
    eng.wait_ge(sem, value)


def attn_moe_kernel(nc, x, w_qkv_t, b_qkv, w_out_t, b_out, w_router, w_gate, w_up, w_down, out):
    B, T, C = x.shape
    E, _, F = w_gate.shape
    FC = F // P
    CH = E * FC
    GROUPS = B * T // GT
    QK = 2 * C
    assert C == P and T == 2 * P and CH == 16 and E == 8 and GROUPS == 16

    x_g = x.rearrange("(g b) (j p) c -> g p (b j) c", g=GROUPS, p=P)
    out_g = out.rearrange("(g b) (j p) c -> g p (b j) c", g=GROUPS, p=P)

    with ExitStack() as ctx:
        def sb(name, shape, dt=F32):
            return ctx.enter_context(nc.sbuf_tensor(name, shape, dt))

        def bank(name):
            return ctx.enter_context(nc.psum_tensor(name, [P, GT], F32))

        def sem(name):
            return ctx.enter_context(nc.semaphore(name))

        ident = sb("ident", [P, P])
        tri_f = sb("tri_f", [P, P])
        ones_f = sb("ones_f", [P, P])
        tri = sb("tri", [P, P], F32R)
        ones = sb("ones", [P, P], F32R)
        sel = sb("sel", [64, E, P], F32R)
        eidx = sb("eidx", [P, TILES, E])
        c_eps = sb("c_eps", [P, 2 * TILES])
        c_mhalf = sb("c_mhalf", [P, 2 * TILES])
        c_3half = sb("c_3half", [P, 2 * TILES])
        c_mone = sb("c_mone", [P, 2 * TILES])
        bias_f = sb("bias_f", [64, 4 * C])
        bias = sb("bias", [64, 4 * C], F32R)

        wqkv_hi = sb("wqkv_hi", [P, 3 * C], F32R)
        wqkv_lo = sb("wqkv_lo", [P, 3 * C], F32R)
        wo_hi = sb("wo_hi", [P, C], F32R)
        wo_lo = sb("wo_lo", [P, C], F32R)
        wr_hi = sb("wr_hi", [P, E], F32R)
        wr_lo = sb("wr_lo", [P, E], F32R)
        wg_hi = sb("wg_hi", [P, E, F], F32R)
        wg_lo = sb("wg_lo", [P, E, F], F32R)
        wu_hi = sb("wu_hi", [P, E, F], F32R)
        wu_lo = sb("wu_lo", [P, E, F], F32R)
        wd_hi = sb("wd_hi", [P, CH, C], F32R)
        wd_lo = sb("wd_lo", [P, CH, C], F32R)
        stage = sb("stage", [P, 3, 2048])

        xin = sb("xin", [P, TILES, C])
        xres = sb("xres", [P, TILES, C])
        xT_hi = sb("xT_hi", [P, GT], F32R)
        xT_lo = sb("xT_lo", [P, GT], F32R)
        z = sb("z", [P, 2, TILES, 3 * C])
        neg = sb("neg", [P, TILES, QK])
        qk = sb("qk", [P, TILES, QK])
        kk_hi = sb("kk_hi", [P, TILES, C], F32R)
        kk_lo = sb("kk_lo", [P, TILES, C], F32R)
        qn = sb("qn", [P, TILES, C])
        nrm = sb("nrm", [P, TILES * HEADS])
        nrm_e = sb("nrm_e", [P, TILES * HEADS])
        rnrm = sb("rnrm", [P, TILES * HEADS])
        qs = sb("qs", [P, TILES, C])
        pf = sb("pf", [P, 4, HALF])
        p_hi = sb("p_hi", [P, 4, HALF], F32R)
        p_lo = sb("p_lo", [P, 4, HALF], F32R)
        w_small = neg[:].rearrange("p j c -> p (j c)")
        wqkv_f, wo_f, wr_f = w_small[:, 0:3 * C], w_small[:, 3 * C:4 * C], w_small[:, 4 * C:4 * C + E]
        sel_f = pf[0:64, 0:2, :].rearrange("p n (e c) -> p (n e) c", c=P)
        zz = sb("zz", [P, 2, HALF])
        ctxt = sb("ctxt", [P, TILES, C])
        cT_hi = sb("cT_hi", [P, GT], F32R)
        cT_lo = sb("cT_lo", [P, GT], F32R)
        r1 = sb("r1", [P, TILES, C])
        x1 = sb("x1", [P, 2, TILES, C])
        x1T_hi = sb("x1T_hi", [P, 2, GT], F32R)
        x1T_lo = sb("x1T_lo", [P, 2, GT], F32R)

        stats = sb("stats", [P, 2 * TILES, 6])
        mv = sb("mv", [P, 2 * TILES, 2])
        nh = sb("nh", [P, 2 * TILES])
        nv = sb("nv", [P, 2 * TILES])
        ny = sb("ny", [P, 2 * TILES])
        na = sb("na", [P, 2 * TILES])
        nm = sb("nm", [P, 2 * TILES])
        nb = sb("nb", [P, 2 * TILES])

        mx = sb("mx", [P, TILES])
        lg = sb("lg", [P, TILES, E])
        ex = sb("ex", [P, TILES, E])
        sm = sb("sm", [P, TILES])
        rs = sb("rs", [P, TILES])
        prob = sb("prob", [P, TILES, E])
        top = sb("top", [P, TILES, 8])
        topi = sb("topi", [P, TILES, 8], U32)
        topf = sb("topf", [P, TILES, 8])
        dlt = sb("dlt", [P, TILES])
        th = sb("th", [P, TILES])
        wk = sb("wk", [P, 2, TILES])
        oh = sb("oh", [P, 2, TILES, E])
        wf = sb("wf", [P, 3, TILES, E])
        wT = sb("wT", [64, 2, GT], F32R)

        wbc = sb("wbc", [P, 2, GT])
        s_act = stage[:, 1, 0:2 * GT].rearrange("p (n t) -> p n t", n=2)
        sw = stage[:, 1, 2 * GT:].rearrange("p (n t) -> p n t", n=2)
        hf = stage[:, 2, 0:2 * GT].rearrange("p (n t) -> p n t", n=2)
        yTs = stage[:, 2, 2 * GT:3 * GT]
        h_hi = sb("h_hi", [P, 4, GT], F32R)
        h_lo = sb("h_lo", [P, 4, GT], F32R)
        r2 = sb("r2", [P, 2, TILES, C])
        res = sb("res", [P, TILES, C])

        GU = [bank(f"GU{n}") for n in range(4)]
        Y = bank("Y")
        CUM = bank("CUM")
        ATT = bank("ATT")
        M = bank("M")

        names = """w_in wg_in wu_in wd_in b_in gp_c0 gp_const dv_const w_hi w_lo w_lo_g wT0
            x_in xres_in x_T xT_hi_d xT_lo_d qkv_d z_d neg_d ex_d qk_d kk_hi_d kk_lo_d cumk_d qn_d nrm_d
            nrme_d rnrm_d qs_d prod_d p_hi_d p_lo_d p_lo_g cum_d zz_d ctx_d ctx_T cT_hi_d cT_lo_d proj_d res_d
            st_d mv1_d mv2_d rn_d x1_d x1_T x1T_hi_d x1T_lo_d logit_d rmax_d lg_d rex_d rchain th_d w_T wT_hi_d
            wT_lo_d wb_d wbs_d g_d u_d silu_d sw_d h_d h_hi_d h_lo_d dn_d yT_d y_T res2_d st2_d
            out_d stored dve_past""".split()
        S = {n: sem(n) for n in names}
        block = ctx.enter_context(nc.Block())

        SPLIT_AT = dict(gate_hi=(-3, 8), up_hi=(-2, 5), down_hi=(-2, 12),
                        up_lo=(-2, 9),
                        gate_lo=(-3, 15), down_lo=(-1, 3))
        RCH = 20
        NEWTON = 17

        def gate_bank(k):
            return GU[(k + 1) % 4]

        def up_bank(k):
            return GU[k % 4]

        def qkv_bank(g, j):
            return (ATT, CUM, Y, M)[j] if isinstance(g, int) and g == 0 else ATT

        LO_VECTOR = 2
        PROD_HEAD, PROD_TAIL = (4.5, 5.5, 6.5, 9.5, 11.5, 12.5, 14.5), (0.5,)
        HI_HEAD, HI_TAIL = (5.5, 6.5, 8.5, 11, 12.5, 13), (0.5, 1.5)
        LO_HEAD, LO_TAIL = (6.5, 9, 10, 10.5, 13, 15.5), (1.5, 2.5)
        CUM_HEAD, CUM_TAIL = (7.5, 9, 10, 11.5, 13.5, 15.5), (1.5, 2.5)
        APPLY_HEAD, APPLY_TAIL = (8.5, 9.5, 11.5, 13, 15.5), (0.5, 2.5, 4)
        PE_AT = dict(x_T=12.5, project_0=14, project_1=15.5, project_2=0, project_3=6, cum_k=4,
                     y_T=4, ctx_T=4, out_project=5.5, x1_T=9.5, logits=11, w_T=14.5, spread_0=15.5)
        SPREAD = (1.5, 3.5, 5.5, 7, 8.5, 11, 13.5)
        ACT_AT = dict(x_hi=13, z_0=14.5, z_1=0, z_2=1.5, z_3=7, neg_0=6.5, neg_1=9.5, exps=11.5, kk_hi=3,
                      y_out=4, ctx_hi=5, layernorm_1=9, x1_hi=10, tanh=13.5, w_hi=15, layernorm_2=15.5)
        DVE_AT = dict(x_lo=13.5, features_0=1.5, features_1=2, kk_lo=3.5, norm_0=4.5, norm_1=5.5, norm_2=7.5,
                      ctx_lo=5.5, res_1=6.5, x1_lo=10.5, logit_max=11.5, router_a=12.5, router_b=14,
                      router_c=14.5, w_lo=15.5, res_2=5.5, stats_2=0.5)
        POOL_AT = dict(rsqrt_a=7.5, rsqrt_b=9)
        DOWN, WEIGH, HIDDEN, HIDDEN_HI, HIDDEN_LO = 4, 1, 2, 2, 3

        def flat(w):
            return w[:].rearrange("p a b -> p (a b)")

        split_gate = (flat(wg_hi), flat(wg_lo), stage[:, 1, :])
        split_up = (flat(wu_hi), flat(wu_lo), stage[:, 2, :])
        split_down = (flat(wd_hi), flat(wd_lo), stage[:, 0, :])

        def lagging(op, lag, s, m, y):
            if s >= lag:
                if m is not None:
                    op(m, s - lag)
            elif y is not None:
                op(y, CH + s - lag)

        def wait_half_lo(eng, h, hs):
            if 0 <= hs < LO_VECTOR:
                wait(eng, S["p_lo_d"], LO_VECTOR * h + hs + 1)
            else:
                wait(eng, S["p_lo_g"], (8 - LO_VECTOR) * h + hs + 1 - (LO_VECTOR if hs > 0 else 0))

        def half_product_lo(eng, subtract, h, hs):
            eng.wait_ge(S["p_hi_d"], 8 * h + hs + 1)
            wait(eng, S["cum_d"], 8 * h + hs - (1 if hs // 2 % 2 == 0 else 3))
            subtract(p_lo[:, hs % 4, :], pf[:, hs % 4, :], p_hi[:, hs % 4, :].bitcast(F32),
                     ALU.subtract).then_inc(S["p_lo_d" if hs < LO_VECTOR else "p_lo_g"], 1)

        def run_units(unit, eng):
            def peeled(u):
                def group(g):
                    return g if 0 <= g < GROUPS else None
                yy = group(u - 2) if u < GROUPS else None
                unit(group(u), u % 2, u + 1, *(group(u + n) for n in (1, 2, 3, 4, -1)), yy)
            for u in range(-4, 4):
                peeled(u)
            with eng.Fori(4, GROUPS - 4, 2) as u:
                unit(u, 0, u + 1, u + 1, u + 2, u + 3, u + 4, u - 1, u - 2)
                unit(u + 1, 1, u + 2, u + 2, u + 3, u + 4, u + 5, u, u - 1)
            for u in range(GROUPS - 4, GROUPS + 1):
                peeled(u)

        def last_y(tail, y):
            return y if tail is None and y is not None and y >= GROUPS - 2 else None

        @block.sync
        def _(sp):
            sp.dma_start(wqkv_f, w_qkv_t).then_inc(S["w_in"], 16)
            sp.dma_start(wo_f, w_out_t).then_inc(S["w_in"], 16)
            sp.dma_start(wr_f, w_router).then_inc(S["w_in"], 16)
            sp.wait_ge(S["gp_c0"], 1)
            for row in (0, 32):
                sp.dma_start(bias_f[row:row + 1, 0:3 * C], b_qkv.rearrange("(o n) -> o n", o=1)).then_inc(S["b_in"], 16)
                sp.dma_start(bias_f[row:row + 1, 3 * C:], b_out.rearrange("(o n) -> o n", o=1)).then_inc(S["b_in"], 16)

            def load(g):
                wait(sp, S["x_T"], g)
                sp.dma_start(xin[:], x_g[g]).then_inc(S["x_in"], 16)

            def load_residual(g):
                wait(sp, S["res_d"], g)
                sp.dma_start(xres[:], x_g[g]).then_inc(S["xres_in"], 16)

            def store(g):
                sp.wait_ge(S["out_d"], (g + 1) * TILES)
                sp.dma_start(out_g[g], res[:]).then_inc(S["stored"], 16)

            load(0)
            sp.dma_start(stage[:, 1, :].rearrange("p (e f) -> p e f", e=E),
                         w_gate.rearrange("e c f -> c e f")).then_inc(S["wg_in"], 16)
            sp.dma_start(stage[:, 2, :].rearrange("p (e f) -> p e f", e=E),
                         w_up.rearrange("e c f -> c e f")).then_inc(S["wu_in"], 16)
            sp.dma_start(stage[:, 0, :].rearrange("p (k c) -> p k c", k=CH),
                         w_down.rearrange("e (k f) c -> f (e k) c", f=P)).then_inc(S["wd_in"], 16)
            load_residual(0)
            load(1)
            load(2)
            for u in (-1, 0, 1):
                load(u + 4)
                load_residual(u + 2)
            with sp.Fori(2, GROUPS - 4) as u:
                load(u + 4)
                load_residual(u + 2)
                store(u - 2)
            for u in range(GROUPS - 4, GROUPS + 2):
                if u + 2 < GROUPS:
                    load_residual(u + 2)
                store(u - 2)
            sp.wait_ge(S["stored"], 16 * GROUPS)

        @block.tensor
        def _(pe):
            mm = nc.tensor.matmul

            def three(dst, a_hi, a_lo, b_hi, b_lo, start=True, stop=True):
                mm(dst, a_hi, b_hi, start=start, stop=False)
                mm(dst, a_hi, b_lo, start=False, stop=False)
                return mm(dst, a_lo, b_hi, start=False, stop=stop)

            def transpose_x(g, tail, pre):
                pe.wait_ge(S["x_in"], 16 * (g + 1))
                if tail is not None:
                    pe.wait_ge(S["lg_d"], tail + 1)
                elif pre is not None:
                    pe.wait_ge(S["z_d"], 4 * pre + 4)
                for j in range(TILES):
                    last = nc.tensor.transpose(ATT[:, j * P:(j + 1) * P], xin[:, j, :], ident[:])
                last.then_inc(S["x_T"], 1)

            def project(g, j, tail):
                if j == 0:
                    pe.wait_ge(S["xT_hi_d"], g + 1)
                    pe.wait_ge(S["xT_lo_d"], g + 1)
                elif j == 3 and tail is not None:
                    pe.wait_ge(S["res_d"], tail + 1)
                elif not isinstance(g, int) or g > 0:
                    pe.wait_ge(S["z_d"], 4 * g + j)
                dst = qkv_bank(g, j)[:, 0:3 * C]
                cols = slice(j * P, (j + 1) * P)
                mm(dst, xT_hi[:, cols], wqkv_hi[:], start=True, stop=False)
                mm(dst, xT_hi[:, cols], wqkv_lo[:], start=False, stop=False)
                mm(dst, xT_lo[:, cols], wqkv_hi[:], start=False, stop=False)
                mm(dst, ones[0:64, :], bias[:, 0:3 * C], start=False, stop=True).then_inc(S["qkv_d"], 1)

            def cumulate_k(h):
                pe.wait_ge(S["kk_hi_d"], h + 1)
                pe.wait_ge(S["kk_lo_d"], h + 1)
                wait(pe, S["zz_d"], 8 * h)
                mm(CUM[:], tri[:], kk_hi[:].rearrange("p j c -> p (j c)"), start=True, stop=False)
                mm(CUM[:], tri[:], kk_lo[:].rearrange("p j c -> p (j c)"), start=False, stop=False)
                second = CUM[:].rearrange("p (b j c) -> p b j c", b=2, j=2)[:, :, 1, :]
                mm(second, ones[:], kk_hi[:].rearrange("p (b j) c -> p b j c", b=2)[:, :, 0, :],
                   start=False, stop=False)
                mm(second, ones[:], kk_lo[:].rearrange("p (b j) c -> p b j c", b=2)[:, :, 0, :],
                   start=False, stop=True).then_inc(S["cumk_d"], 1)

            def cumulate(h, hs):
                pe.wait_ge(S["p_hi_d"], 8 * h + hs + 1)
                wait_half_lo(pe, h, hs)
                if hs == 0:
                    pe.wait_ge(S["qn_d"], h + 1)
                else:
                    pe.wait_ge(S["zz_d"], 8 * h + hs)
                second = (hs // 2) % 2 == 1
                mm(CUM[:], tri[:], p_hi[:, hs % 4, :], start=True, stop=False)
                last = mm(CUM[:], tri[:], p_lo[:, hs % 4, :], start=False, stop=not second)
                if second:
                    mm(CUM[:], ones[:], p_hi[:, (hs - 2) % 4, :], start=False, stop=False)
                    last = mm(CUM[:], ones[:], p_lo[:, (hs - 2) % 4, :], start=False, stop=True)
                last.then_inc(S["cum_d"], 1)

            def transpose_ctx(t, pre):
                if pre is not None:
                    pe.wait_ge(S["z_d"], 4 * pre + 3)
                else:
                    pe.wait_ge(S["lg_d"], t)
                pe.wait_ge(S["ctx_d"], 8 * (t + 1))
                for j in range(TILES):
                    last = nc.tensor.transpose(ATT[:, j * P:(j + 1) * P], ctxt[:, j, :], ident[:])
                last.then_inc(S["ctx_T"], 1)

            def out_project(t):
                pe.wait_ge(S["cT_hi_d"], t + 1)
                pe.wait_ge(S["cT_lo_d"], t + 1)
                for j in range(TILES):
                    cols = slice(j * P, (j + 1) * P)
                    three(ATT[:, cols], cT_hi[:, cols], cT_lo[:, cols], wo_hi[:], wo_lo[:], stop=False)
                    last = mm(ATT[:, cols], ones[0:64, :], bias[:, 3 * C:], start=False, stop=True)
                last.then_inc(S["proj_d"], 1)

            def transpose_x1(t, par, pre):
                pe.wait_ge(S["x1_d"], TILES * (t + 1))
                if pre is not None:
                    pe.wait_ge(S["z_d"], 4 * pre + 4)
                else:
                    pe.wait_ge(S["res_d"], t + 1)
                for j in range(TILES):
                    last = nc.tensor.transpose(ATT[:, j * P:(j + 1) * P], x1[:, par, j, :], ident[:])
                last.then_inc(S["x1_T"], 1)

            def logits(t, par):
                pe.wait_ge(S["x1T_hi_d"], t + 1)
                pe.wait_ge(S["x1T_lo_d"], t + 1)
                for j in range(TILES):
                    cols = slice(j * P, (j + 1) * P)
                    last = three(ATT[:, j * E:(j + 1) * E], x1T_hi[:, par, cols], x1T_lo[:, par, cols],
                                 wr_hi[:], wr_lo[:])
                last.then_inc(S["logit_d"], 1)

            def transpose_w(t, m):
                pe.wait_ge(S["rchain"], RCH * (t + 1))
                if m is not None:
                    pe.wait_ge(S["wbs_d"], E * (m + 1))
                for j in range(TILES):
                    last = nc.tensor.transpose(M[0:E, j * P:(j + 1) * P], wf[:, 2, j, :], ident[:])
                last.then_inc(S["w_T"], 1)

            def transpose_y(y, m):
                pe.wait_ge(S["yT_d"], y + 1)
                if m is not None:
                    pe.wait_ge(S["wbs_d"], E * m + 3)
                for j in range(TILES):
                    last = nc.tensor.transpose(M[:, j * P:(j + 1) * P], yTs[:, j * P:(j + 1) * P], ident[:])
                last.then_inc(S["y_T"], 1)

            def spread(m, par, e, y):
                if e == 0:
                    pe.wait_ge(S["wT0"], 1)
                    pe.wait_ge(S["wT_hi_d"], m + 1)
                    pe.wait_ge(S["wT_lo_d"], m + 1)
                else:
                    pe.wait_ge(S["wbs_d"], E * m + e)
                if e == 3 and y is not None:
                    pe.wait_ge(S["res2_d"], y + 1)
                mm(M[:], sel[:, e, :], wT[:, par, :], start=True, stop=True).then_inc(S["wb_d"], 1)

            def gate_up(m, par, k):
                n = CH * m + k
                if k == 0:
                    pe.wait_ge(S["x1T_hi_d"], m + 1)
                    pe.wait_ge(S["x1T_lo_d"], m + 1)
                e, f = k // FC, slice(k % FC * P, (k % FC + 1) * P)
                wait(pe, S["h_d"], n - 2)
                three(gate_bank(k)[:], wg_hi[:, e, f], wg_lo[:, e, f], x1T_hi[:, par, :],
                      x1T_lo[:, par, :]).then_inc(S["g_d"], 1)
                wait(pe, S["silu_d"], n)
                three(up_bank(k)[:], wu_hi[:, e, f], wu_lo[:, e, f], x1T_hi[:, par, :],
                      x1T_lo[:, par, :]).then_inc(S["u_d"], 1)

            def down(m, k):
                n = CH * m + k
                pe.wait_ge(S["h_hi_d"], n + 1)
                pe.wait_ge(S["h_lo_d"], n + 1)
                if k == 0:
                    wait(pe, S["yT_d"], m)
                three(Y[:], wd_hi[:, k, :], wd_lo[:, k, :], h_hi[:, k % 4, :], h_lo[:, k % 4, :],
                      start=(k == 0), stop=(k == CH - 1)).then_inc(S["dn_d"], 1)

            def step(s, m, par, tail, head, pre, nxt, y):
                at = PE_AT
                if s in SPREAD and m is not None:
                    spread(m, par, SPREAD.index(s) + 1, y)
                for j in (2, 3):
                    if s == at[f"project_{j}"] and pre is not None:
                        project(pre, j, tail)
                if s == at["cum_k"] and head is not None:
                    cumulate_k(head)
                if s == at["y_T"] and y is not None:
                    transpose_y(y, m)
                if s == at["ctx_T"] and tail is not None:
                    transpose_ctx(tail, pre)
                if s == at["out_project"] and tail is not None:
                    out_project(tail)
                if s == at["x1_T"] and tail is not None:
                    transpose_x1(tail, 1 - par, pre)
                if s == at["logits"] and tail is not None:
                    logits(tail, 1 - par)
                if s == at["x_T"] and nxt is not None:
                    transpose_x(nxt, tail, pre)
                for j in (0, 1):
                    if s == at[f"project_{j}"] and nxt is not None:
                        project(nxt, j, None)
                if s == at["w_T"] and tail is not None:
                    transpose_w(tail, m)
                if s == at["spread_0"] and tail is not None:
                    spread(tail, 1 - par, 0, None)
                if s in CUM_HEAD and head is not None:
                    cumulate(head, CUM_HEAD.index(s))
                if s in CUM_TAIL and tail is not None:
                    cumulate(tail, len(CUM_HEAD) + CUM_TAIL.index(s))

            def unit(m, par, idx, tail, head, pre, nxt, y, yy):
                for s in range(CH):
                    if m is not None:
                        if isinstance(m, int) and m == 0 and s == 0:
                            pe.wait_ge(S["w_hi"], 7)
                            pe.wait_ge(S["w_lo"], 5)
                            pe.wait_ge(S["w_lo_g"], 2)
                        gate_up(m, par, s)
                    step(s, m, par, tail, head, pre, nxt, y)
                    lagging(down, DOWN, s, m, y)
                    step(s + 0.5, m, par, tail, head, pre, nxt, y)

            pe.wait_ge(S["gp_const"], 3)
            pe.wait_ge(S["dv_const"], 3)
            pe.wait_ge(S["w_hi"], 4)
            pe.wait_ge(S["w_lo"], 4)
            run_units(unit, pe)

        @block.scalar
        def _(act):
            def copy(dst, src):
                return nc.scalar.activation(dst, src, ACT.Copy)

            def z_copy(g, j, par):
                act.wait_ge(S["qkv_d"], 4 * g + j + 1)
                wait(act, S["prod_d"], 8 * (g - 2) + 2 * j + 2)
                copy(z[:, par, j, :], qkv_bank(g, j)[:, 0:3 * C]).then_inc(S["z_d"], 1)

            def negative_part(g, b, par):
                two = slice(2 * b, 2 * b + 2)
                act.wait_ge(S["z_d"], 4 * g + 2 * b + 2)
                wait(act, S["qk_d"], 2 * g + b - 1)
                nc.scalar.activation(neg[:, two, :], z[:, par, two, 0:QK], ACT.Relu,
                                     scale=-1.0).then_inc(S["neg_d"], 1)

            def product_hi(h, hs):
                act.wait_ge(S["prod_d"], 8 * h + hs + 1)
                wait(act, S["cum_d"], 8 * h + hs - (1 if hs // 2 % 2 == 0 else 3))
                copy(p_hi[:, hs % 4, :], pf[:, hs % 4, :]).then_inc(S["p_hi_d"], 1)

            def silu(m, k):
                n = CH * m + k
                act.wait_ge(S["g_d"], n + 1)
                wait(act, S["sw_d"], n - 1)
                nc.scalar.activation(s_act[:, k % 2, :], gate_bank(k)[:], ACT.Silu).then_inc(S["silu_d"], 1)

            def hidden_hi(m, k):
                n = CH * m + k
                act.wait_ge(S["h_d"], n + 1)
                wait(act, S["dn_d"], n - 3)
                copy(h_hi[:, k % 4, :], hf[:, k % 2, :]).then_inc(S["h_hi_d"], 1)

            def weights_out(m, e):
                act.wait_ge(S["wb_d"], E * m + e + 1)
                wait(act, S["sw_d"], CH * m + FC * (e - 1))
                copy(wbc[:, e % 2, :], M[:]).then_inc(S["wbs_d"], 1)

            def x_hi(h):
                act.wait_ge(S["x_T"], h + 1)
                wait(act, S["qkv_d"], 4 * h)
                copy(xT_hi[:], ATT[:]).then_inc(S["xT_hi_d"], 1)

            def normalize(idx, first, src, dst, done):
                act.wait_ge(S["rn_d"], NEWTON * (idx + 1))
                for j in range(TILES):
                    at = slice(first + j, first + j + 1)
                    nc.scalar.activation(dst[:, j, :], src[:, j, :], ACT.Identity, bias=nb[:, at],
                                         scale=ny[:, at]).then_inc(done, 1)

            def step(s, m, par, idx, tail, head, pre, nxt, y, yy):
                at = ACT_AT
                if s % FC == 0 and m is not None:
                    weights_out(m, int(s) // FC)
                for j in (1, 2, 3):
                    if s == at[f"z_{j}"] and pre is not None:
                        z_copy(pre, j, 1 - par)
                if s == at["kk_hi"] and head is not None:
                    act.wait_ge(S["qk_d"], 2 * head + 2)
                    wait(act, S["cumk_d"], head)
                    copy(kk_hi[:], qk[:, :, C:QK]).then_inc(S["kk_hi_d"], 1)
                if s == at["y_out"] and y is not None:
                    act.wait_ge(S["dn_d"], CH * (y + 1))
                    wait(act, S["y_T"], y)
                    copy(yTs, Y[:]).then_inc(S["yT_d"], 1)
                if s == at["ctx_hi"] and tail is not None:
                    act.wait_ge(S["ctx_T"], tail + 1)
                    wait(act, S["proj_d"], tail)
                    copy(cT_hi[:], ATT[:]).then_inc(S["cT_hi_d"], 1)
                if s == at["layernorm_1"] and tail is not None:
                    wait(act, S["x1_T"], tail - 1)
                    wait(act, S["res2_d"], tail - 1)
                    normalize(idx, 0, r1, x1[:, 1 - par], S["x1_d"])
                if s == at["x1_hi"] and tail is not None:
                    act.wait_ge(S["x1_T"], tail + 1)
                    if not isinstance(tail, int) or tail >= 2:
                        act.wait_ge(S["u_d"], CH * (tail - 1))
                        act.wait_ge(S["logit_d"], tail)
                    copy(x1T_hi[:, 1 - par, :], ATT[:]).then_inc(S["x1T_hi_d"], 1)
                if s == at["x_hi"] and nxt is not None:
                    x_hi(nxt)
                if s == at["z_0"] and nxt is not None:
                    z_copy(nxt, 0, par)
                if s == at["w_hi"] and tail is not None:
                    act.wait_ge(S["w_T"], tail + 1)
                    wait(act, S["wb_d"], E * (tail - 1))
                    copy(wT[0:E, 1 - par, :], M[0:E, :]).then_inc(S["wT_hi_d"], 1)
                for slots, g, first in ((HI_HEAD, head, 0), (HI_TAIL, tail, len(HI_HEAD))):
                    if s in slots and g is not None:
                        product_hi(g, first + slots.index(s))
                for b in (0, 1):
                    if s == at[f"neg_{b}"] and pre is not None:
                        negative_part(pre, b, 1 - par)
                if s == at["exps"] and pre is not None:
                    act.wait_ge(S["neg_d"], 2 * pre + 2)
                    nc.scalar.activation(neg[:], neg[:], ACT.Exp, scale=-1.0).then_inc(S["ex_d"], 1)
                if s == at["exps"] and tail is not None:
                    act.wait_ge(S["lg_d"], tail + 1)
                    wait(act, S["rchain"], RCH * tail)
                    nc.scalar.activation(ex[:], lg[:], ACT.Exp).then_inc(S["rex_d"], 1)
                if s == at["tanh"] and tail is not None:
                    act.wait_ge(S["rchain"], RCH * tail + 8)
                    nc.scalar.activation(th[:], dlt[:], ACT.Tanh, scale=0.5).then_inc(S["th_d"], 1)
                last = last_y(tail, y)
                if s == (at["layernorm_2"] if last is None else at["layernorm_2"] - 4) and yy is not None:
                    wait(act, S["stored"], 16 * yy)
                    normalize(idx, TILES, r2[:, par], res, S["out_d"])
                if s == at["layernorm_2"] and last is not None:
                    act.wait_ge(S["stored"], 16 * last)
                    normalize(idx, 0, r2[:, 1 - par], res, S["out_d"])
                for what, loaded, (hi, lo, raw) in (("gate_hi", "wg_in", split_gate), ("up_hi", "wu_in", split_up),
                                                    ("down_hi", "wd_in", split_down)):
                    if isinstance(idx, int) and (idx - 1, s) == SPLIT_AT[what]:
                        act.wait_ge(S[loaded], 16)
                        copy(hi, raw).then_inc(S["w_hi"], 1)

            def unit(m, par, idx, tail, head, pre, nxt, y, yy):
                for s in range(CH):
                    step(s, m, par, idx, tail, head, pre, nxt, y, yy)
                    if m is not None:
                        silu(m, s)
                    lagging(hidden_hi, HIDDEN_HI, s, m, y)
                    step(s + 0.5, m, par, idx, tail, head, pre, nxt, y, yy)

            act.wait_ge(S["w_in"], 48)
            copy(wqkv_hi[:], wqkv_f).then_inc(S["w_hi"], 1)
            copy(wo_hi[:], wo_f).then_inc(S["w_hi"], 1)
            copy(wr_hi[:], wr_f).then_inc(S["w_hi"], 1)
            act.wait_ge(S["b_in"], 64)
            copy(bias[0:32, :], bias_f[0:32, :]).then_inc(S["w_hi"], 1)
            run_units(unit, act)

        @block.vector
        def _(dve):
            tt = nc.vector.tensor_tensor
            ts = nc.vector.tensor_scalar

            def low(dst, src, hi):
                return tt(dst, src, hi.bitcast(F32), ALU.subtract)

            def hidden(m, k):
                n = CH * m + k
                dve.wait_ge(S["sw_d"], n + 1)
                dve.wait_ge(S["u_d"], n + 1)
                wait(dve, S["h_hi_d"], n - 1)
                wait(dve, S["h_lo_d"], n - 1)
                tt(hf[:, k % 2, :], up_bank(k)[:], sw[:, k % 2, :], ALU.mult).then_inc(S["h_d"], 1)

            def hidden_lo(m, k):
                n = CH * m + k
                dve.wait_ge(S["h_hi_d"], n + 1)
                wait(dve, S["dn_d"], n - 3)
                low(h_lo[:, k % 4, :], hf[:, k % 2, :], h_hi[:, k % 4, :]).then_inc(S["h_lo_d"], 1)

            def statistics(idx, g, first, src, st, done):
                wait(dve, done, TILES * g)
                for j in range(TILES):
                    nc.vector.bn_stats(stats[:, first + j, :], src[:, j, :]).then_inc(st, 1)
                wait(dve, S["rn_d"], NEWTON * idx)
                dve.wait_ge(st, TILES * (g + 1))
                dve.sem_inc(S["dve_past"], 1)
                for j in range(TILES):
                    nc.vector.bn_aggr(mv[:, first + j, :], stats[:, first + j, :]).then_inc(done, 1)

            def apply_q(h, hs):
                j, half = hs // 2, hs % 2
                dve.wait_ge(S["cum_d"], 8 * h + hs + 1)
                dve.wait_ge(S["qs_d"], h + 1)
                wait(dve, S["ctx_d"], 8 * h + hs - 1)
                q4 = qs[:, j, half * 64:(half + 1) * 64].rearrange("p (h o d) -> p h o d", o=1, d=D)
                tt(zz[:, hs % 2, :].rearrange("p (h e d) -> p h e d", e=D, d=D),
                   CUM[:].rearrange("p (h e d) -> p h e d", e=D, d=D),
                   q4.to_broadcast([P, HEADS // 2, D, D]), ALU.mult).then_inc(S["zz_d"], 1)

            def contract(h, hs):
                j, half = hs // 2, hs % 2
                dve.wait_ge(S["zz_d"], 8 * h + hs + 1)
                wait(dve, S["ctx_T"], h)
                nc.vector.tensor_reduce(ctxt[:, j, half * 64:(half + 1) * 64],
                                        zz[:, hs % 2, :].rearrange("p (c d) -> p c d", d=D),
                                        AX_X, ALU.add).then_inc(S["ctx_d"], 1)

            def bc(v):
                return v.rearrange("p (j o) -> p j o", o=1).to_broadcast([P, TILES, E])

            def router(t, a, b):
                base = RCH * t
                c = S["rchain"]

                def after(n):
                    wait(dve, c, base + n)
                def s1():
                    dve.wait_ge(S["rex_d"], t + 1)
                    return nc.vector.tensor_reduce(sm[:], ex[:], AX_X, ALU.add)
                def s2():
                    after(1)
                    return nc.vector.reciprocal(rs[:], sm[:])
                def s3():
                    after(2)
                    return tt(prob[:], ex[:], bc(rs[:]), ALU.mult)
                def s_max(j):
                    def s():
                        if j == 0:
                            after(3)
                            dve.sem_inc(S["dve_past"], 1)
                        return nc.vector.max(top[:, j, :], prob[:, j, :])
                    return s
                def s_idx(j):
                    def s():
                        if j == 0:
                            after(7)
                            dve.sem_inc(S["dve_past"], 1)
                        return nc.vector.max_index(topi[:, j, :], top[:, j, :], prob[:, j, :])
                    return s
                def s_diff():
                    after(7)
                    wait(dve, S["th_d"], t)
                    return tt(dlt[:], top[:, :, 0], top[:, :, 1], ALU.subtract)
                def s13():
                    after(12)
                    return nc.vector.tensor_copy(topf[:], topi[:])
                def s14():
                    dve.wait_ge(S["th_d"], t + 1)
                    return ts(wk[:, 0, :], th[:], 0.5, 0.5, ALU.mult, ALU.add)
                def s15():
                    return ts(wk[:, 1, :], th[:], -0.5, 0.5, ALU.mult, ALU.add)
                def s_oh(n):
                    def s():
                        after(13)
                        return tt(oh[:, n], eidx[:], bc(topf[:, :, n]), ALU.is_equal)
                    return s
                def s_w(n):
                    def s():
                        after(16 + n)
                        return tt(wf[:, n], oh[:, n], bc(wk[:, n, :]), ALU.mult)
                    return s
                def s20():
                    after(19)
                    wait(dve, S["w_T"], t)
                    return tt(wf[:, 2], wf[:, 0], wf[:, 1], ALU.add)
                steps = ([s1, s2, s3] + [s_max(j) for j in range(TILES)] + [s_diff]
                         + [s_idx(j) for j in range(TILES)] + [s13, s14, s15, s_oh(0), s_oh(1), s_w(0), s_w(1), s20])
                for n in range(a, b + 1):
                    steps[n - 1]().then_inc(c, 1)

            def x_lo(h):
                dve.wait_ge(S["xT_hi_d"], h + 1)
                wait(dve, S["qkv_d"], 4 * h)
                low(xT_lo[:], ATT[:], xT_hi[:]).then_inc(S["xT_lo_d"], 1)

            def features(h, b, par):
                two = slice(2 * b, 2 * b + 2)
                dve.wait_ge(S["ex_d"], h + 1)
                wait(dve, S["prod_d"], 8 * h - 4 + 4 * b)
                if b == 0:
                    wait(dve, S["qs_d"], h)
                    wait(dve, S["kk_lo_d"], h)
                    wait(dve, S["kk_hi_d"], h)
                nc.vector.scalar_tensor_tensor(out=qk[:, two, :], in0=z[:, par, two, 0:QK], scalar=0.0,
                                               in1=neg[:, two, :], op0=ALU.max, op1=ALU.add).then_inc(S["qk_d"], 1)

            def residual_1(t):
                dve.wait_ge(S["proj_d"], t + 1)
                dve.wait_ge(S["xres_in"], 16 * (t + 1))
                wait(dve, S["x1_d"], TILES * t)
                tt(r1[:].rearrange("p j c -> p (j c)"), ATT[:], xres[:].rearrange("p j c -> p (j c)"),
                   ALU.add).then_inc(S["res_d"], 1)

            def residual_2(y, par):
                dve.wait_ge(S["y_T"], y + 1)
                wait(dve, S["out_d"], TILES * (y - 1))
                tt(r2[:, par].rearrange("p j c -> p (j c)"), M[:],
                   x1[:, par].rearrange("p j c -> p (j c)"), ALU.add).then_inc(S["res2_d"], 1)

            def norm(h, part):
                if part == 0:
                    dve.wait_ge(S["cumk_d"], h + 1)
                    wait(dve, S["nrm_d"], h)
                    tt(qn[:], CUM[:].rearrange("p (j c) -> p j c", c=C), qk[:, :, 0:C],
                       ALU.mult).then_inc(S["qn_d"], 1)
                if part == 1:
                    dve.wait_ge(S["qn_d"], h + 1)
                    nc.vector.tensor_reduce(nrm[:], qn[:].rearrange("p j (h d) -> p (j h) d", d=D),
                                            AX_X, ALU.add).then_inc(S["nrm_d"], 1)
                if part == 2:
                    dve.wait_ge(S["nrm_d"], h + 1)
                    ts(nrm_e[:], nrm[:], EPS_NORM, None, ALU.add).then_inc(S["nrme_d"], 1)
                    dve.wait_ge(S["nrme_d"], h + 1)
                    nc.vector.reciprocal(rnrm[:], nrm_e[:]).then_inc(S["rnrm_d"], 1)
                    dve.wait_ge(S["rnrm_d"], h + 1)
                    wait(dve, S["zz_d"], 8 * h)
                    tt(qs[:].rearrange("p j (h d) -> p j h d", d=D),
                       qk[:, :, 0:C].rearrange("p j (h d) -> p j h d", d=D),
                       rnrm[:].rearrange("p (j h o) -> p j h o", o=1, h=HEADS).to_broadcast([P, TILES, HEADS, D]),
                       ALU.mult).then_inc(S["qs_d"], 1)

            def half(h, hs):
                apply_q(h, hs)
                contract(h, hs)

            def logit_max(t):
                dve.wait_ge(S["logit_d"], t + 1)
                lg3 = ATT[:, 0:TILES * E].rearrange("p (j e) -> p j e", e=E)
                wait(dve, S["lg_d"], t)
                nc.vector.tensor_reduce(mx[:], lg3, AX_X, ALU.max).then_inc(S["rmax_d"], 1)
                dve.wait_ge(S["rmax_d"], t + 1)
                wait(dve, S["rex_d"], t)
                tt(lg[:], lg3, bc(mx[:]), ALU.subtract).then_inc(S["lg_d"], 1)

            def step(s, m, par, idx, tail, head, pre, nxt, y, yy):
                at = DVE_AT
                for hs in range(LO_VECTOR):
                    if s == LO_HEAD[hs] and head is not None:
                        half_product_lo(dve, tt, head, hs)
                for slots, g, first in ((APPLY_HEAD, head, 0), (APPLY_TAIL, tail, len(APPLY_HEAD))):
                    if s in slots and g is not None:
                        half(g, first + slots.index(s))
                for b in (0, 1):
                    if s == at[f"features_{b}"] and head is not None:
                        features(head, b, par)
                if s == at["stats_2"] and yy is not None:
                    dve.wait_ge(S["res2_d"], yy + 1)
                    statistics(idx, yy, TILES, r2[:, par], S["st2_d"], S["mv2_d"])
                if s == at["kk_lo"] and head is not None:
                    dve.wait_ge(S["kk_hi_d"], head + 1)
                    wait(dve, S["cumk_d"], head)
                    low(kk_lo[:], qk[:, :, C:QK], kk_hi[:]).then_inc(S["kk_lo_d"], 1)
                if s == at["res_2"] and y is not None:
                    residual_2(y, 1 - par)
                    if last_y(tail, y) is not None:
                        dve.wait_ge(S["res2_d"], y + 1)
                        statistics(idx, y, 0, r2[:, 1 - par], S["st2_d"], S["mv2_d"])
                if isinstance(idx, int) and (idx - 1, s) == SPLIT_AT["up_lo"]:
                    hi, lo, raw = split_up
                    dve.wait_ge(S["w_hi"], 6)
                    low(lo, raw, hi).then_inc(S["w_lo"], 1)
                if s == at["ctx_lo"] and tail is not None:
                    dve.wait_ge(S["cT_hi_d"], tail + 1)
                    wait(dve, S["proj_d"], tail)
                    low(cT_lo[:], ATT[:], cT_hi[:]).then_inc(S["cT_lo_d"], 1)
                if s == at["res_1"] and tail is not None:
                    residual_1(tail)
                    dve.wait_ge(S["res_d"], tail + 1)
                    statistics(idx, tail, 0, r1, S["st_d"], S["mv1_d"])
                for n in (0, 1, 2):
                    if s == at[f"norm_{n}"] and head is not None:
                        norm(head, n)
                if s == at["x1_lo"] and tail is not None:
                    dve.wait_ge(S["x1T_hi_d"], tail + 1)
                    if not isinstance(tail, int) or tail >= 2:
                        dve.wait_ge(S["u_d"], CH * (tail - 1))
                        dve.wait_ge(S["logit_d"], tail)
                    low(x1T_lo[:, 1 - par, :], ATT[:], x1T_hi[:, 1 - par, :]).then_inc(S["x1T_lo_d"], 1)
                if s == at["logit_max"] and tail is not None:
                    logit_max(tail)
                for part, a, b in ("a", 1, 8), ("b", 9, 13), ("c", 14, 20):
                    if s == at[f"router_{part}"] and tail is not None:
                        router(tail, a, b)
                if s == at["x_lo"] and nxt is not None:
                    x_lo(nxt)
                if s == at["w_lo"] and tail is not None:
                    dve.wait_ge(S["wT_hi_d"], tail + 1)
                    wait(dve, S["wb_d"], E * (tail - 1))
                    low(wT[32:32 + E, 1 - par, :], M[0:E, :], wT[0:E, 1 - par, :]).then_inc(S["wT_lo_d"], 1)

            def unit(m, par, idx, tail, head, pre, nxt, y, yy):
                for s in range(CH):
                    step(s, m, par, idx, tail, head, pre, nxt, y, yy)
                    lagging(hidden_lo, HIDDEN_LO, s, m, y)
                    lagging(hidden, HIDDEN, s, m, y)
                    step(s + 0.5, m, par, idx, tail, head, pre, nxt, y, yy)

            dve.wait_ge(S["gp_const"], 3)
            nc.vector.tensor_copy(tri[:], tri_f[:]).then_inc(S["dv_const"], 1)
            nc.vector.tensor_copy(ones[:], ones_f[:]).then_inc(S["dv_const"], 1)
            nc.vector.tensor_copy(sel[:].rearrange("p e c -> p (e c)"),
                                  sel_f[:].rearrange("p e c -> p (e c)")).then_inc(S["dv_const"], 1)
            nc.vector.memset(wT[:].bitcast(F32), 0.0).then_inc(S["wT0"], 1)
            dve.wait_ge(S["wT0"], 1)
            dve.wait_ge(S["w_hi"], 4)
            low(wqkv_lo[:], wqkv_f, wqkv_hi[:]).then_inc(S["w_lo"], 1)
            low(wo_lo[:], wo_f, wo_hi[:]).then_inc(S["w_lo"], 1)
            low(wr_lo[:], wr_f, wr_hi[:]).then_inc(S["w_lo"], 1)
            low(bias[32:64, :], bias_f[0:32, :], bias[0:32, :]).then_inc(S["w_lo"], 1)
            run_units(unit, dve)

        @block.gpsimd
        def _(pool):
            gtt = nc.gpsimd.tensor_tensor
            gts = nc.gpsimd.tensor_scalar

            def weigh(m, k):
                n = CH * m + k
                pool.wait_ge(S["silu_d"], n + 1)
                pool.wait_ge(S["wbs_d"], E * m + k // FC + 1)
                wait(pool, S["h_d"], n - 1)
                gtt(sw[:, k % 2, :], s_act[:, k % 2, :], wbc[:, (k // FC) % 2, :], ALU.mult).then_inc(S["sw_d"], 1)

            def half_product(h, hs, par):
                j, side = hs // 2, hs % 2
                pool.wait_ge(S["qk_d"], 2 * h + hs // 4 + 1)
                if hs == 0:
                    pool.wait_ge(S["dv_const"], 3)
                wait(pool, S["p_hi_d"], 8 * h + hs - 3)
                wait_half_lo(pool, h, hs - 4)
                k0, v0 = C + side * 64, QK + side * 64
                k4 = qk[:, j, k0:k0 + 64].rearrange("p (h o d) -> p h o d", o=1, d=D)
                v4 = z[:, par, j, v0:v0 + 64].rearrange("p (h e o) -> p h e o", o=1, e=D)
                shape = [P, HEADS // 2, D, D]
                gtt(pf[:, hs % 4, :].rearrange("p (h e d) -> p h e d", e=D, d=D), k4.to_broadcast(shape),
                    v4.to_broadcast(shape), ALU.mult).then_inc(S["prod_d"], 1)

            def rsqrt(idx, tail, yy, done, part):
                c = S["rn_d"]
                v, vh, y, a = nv[:], nh[:], ny[:], na[:]
                base = NEWTON * idx
                if part == 0:
                    if tail is not None:
                        pool.wait_ge(S["mv1_d"], TILES * (tail + 1))
                        wait(pool, S["x1_d"], TILES * tail)
                    if yy is not None:
                        pool.wait_ge(S["mv2_d"], TILES * (yy + 1))
                        wait(pool, S["out_d"], TILES * done)
                    gtt(v, mv[:, :, 1], c_eps[:], ALU.add).then_inc(c, 1)
                    gtt(nm[:], mv[:, :, 0], c_mone[:], ALU.mult).then_inc(c, 1)
                    pool.wait_ge(c, base + 1)
                    gtt(vh, v, c_mhalf[:], ALU.mult).then_inc(c, 1)
                    gts(y.bitcast(I32), v.bitcast(I32), -0.5, RSQRT_MAGIC, ALU.mult, ALU.add).then_inc(c, 1)
                for n in ((0,), (1, 2))[part]:
                    at = 4 + 4 * n
                    pool.wait_ge(c, base + at)
                    gtt(a, y, y, ALU.mult).then_inc(c, 1)
                    pool.wait_ge(c, base + at + 1)
                    gtt(a, a, vh, ALU.mult).then_inc(c, 1)
                    pool.wait_ge(c, base + at + 2)
                    gtt(a, a, c_3half[:], ALU.add).then_inc(c, 1)
                    pool.wait_ge(c, base + at + 3)
                    gtt(y, y, a, ALU.mult).then_inc(c, 1)
                if part == 1:
                    pool.wait_ge(c, base + NEWTON - 1)
                    gtt(nb[:], nm[:], y, ALU.mult).then_inc(c, 1)

            def step(s, m, par, idx, tail, head, y, yy):
                for what, n, (hi, lo, raw) in ("gate_lo", 5, split_gate), ("down_lo", 7, split_down):
                    if isinstance(idx, int) and (idx - 1, s) == SPLIT_AT[what]:
                        pool.wait_ge(S["w_hi"], n)
                        gtt(lo, raw, hi.bitcast(F32), ALU.subtract).then_inc(S["w_lo_g"], 1)
                for part, slot in enumerate((POOL_AT["rsqrt_a"], POOL_AT["rsqrt_b"])):
                    last = last_y(tail, y)
                    if s == slot and last is not None:
                        rsqrt(idx, tail, last, last if yy is None else yy, part)
                    elif s == slot and (tail is not None or yy is not None):
                        rsqrt(idx, tail, yy, yy, part)
                for slots, g, first in ((LO_HEAD, head, 0), (LO_TAIL, tail, len(LO_HEAD))):
                    for n, at in enumerate(slots):
                        if s == at and first + n >= LO_VECTOR and g is not None:
                            half_product_lo(pool, gtt, g, first + n)
                for slots, g, first, p in ((PROD_HEAD, head, 0, par), (PROD_TAIL, tail, len(PROD_HEAD), 1 - par)):
                    if s in slots and g is not None:
                        half_product(g, first + slots.index(s), p)

            def unit(m, par, idx, tail, head, pre, nxt, y, yy):
                for s in range(CH):
                    step(s, m, par, idx, tail, head, y, yy)
                    lagging(weigh, WEIGH, s, m, y)
                    step(s + 0.5, m, par, idx, tail, head, y, yy)

            nc.gpsimd.memset(bias_f[:], 0.0).then_inc(S["gp_c0"], 1)
            nc.gpsimd.memset(ident[:], 0.0).then_inc(S["gp_c0"], 1)
            nc.gpsimd.memset(tri_f[:], 1.0).then_inc(S["gp_c0"], 1)
            nc.gpsimd.memset(sel_f[:], 0.0).then_inc(S["gp_c0"], 1)
            nc.gpsimd.memset(ones_f[:], 1.0).then_inc(S["gp_c0"], 1)
            nc.gpsimd.iota(eidx[:], pattern=[[0, TILES], [1, E]], base=0, channel_multiplier=0,
                           allow_small_or_imprecise_dtypes=True).then_inc(S["gp_c0"], 1)
            nc.gpsimd.memset(c_eps[:], EPS_LN).then_inc(S["gp_c0"], 1)
            nc.gpsimd.memset(c_mhalf[:], -0.5).then_inc(S["gp_c0"], 1)
            nc.gpsimd.memset(c_3half[:], 1.5).then_inc(S["gp_c0"], 1)
            nc.gpsimd.memset(c_mone[:], -1.0).then_inc(S["gp_c0"], 1)
            nc.gpsimd.memset(mv[:], 0.0).then_inc(S["gp_c0"], 1)
            pool.wait_ge(S["gp_c0"], 11)
            nc.gpsimd.affine_select(out=sel_f[:], in_=sel_f[:], compare_op=ALU.not_equal, fill=1.0, base=0,
                                    pattern=[[-1, E], [0, P]], channel_multiplier=1).then_inc(S["gp_c0"], 1)
            nc.gpsimd.affine_select(out=ident[:], in_=ident[:], compare_op=ALU.not_equal, fill=1.0, base=0,
                                    pattern=[[-1, P]], channel_multiplier=1).then_inc(S["gp_const"], 1)
            nc.gpsimd.affine_select(out=tri_f[:], in_=tri_f[:], compare_op=ALU.is_ge, fill=0.0, base=0,
                                    pattern=[[1, P]], channel_multiplier=-1).then_inc(S["gp_const"], 1)
            pool.wait_ge(S["gp_c0"], 12)
            nc.gpsimd.affine_select(out=sel_f[:], in_=sel_f[:], compare_op=ALU.not_equal, fill=1.0, base=-32,
                                    pattern=[[-1, E], [0, P]], channel_multiplier=1).then_inc(S["gp_const"], 1)
            run_units(unit, pool)


def kernel(L0_attn_x, L0_attn_w_qkv, L0_attn_b_qkv, L0_attn_w_out, L0_attn_b_out, L0_ffn_router_kernel_DE,
           L0_ffn_kernel_gating_EDF, L0_ffn_kernel_up_EDF, L0_ffn_kernel_down_EFD):
    import numpy as np
    import concourse.bacc as bacc
    from concourse import mybir
    from concourse.bass_utils import run_bass_kernel_spmd as run

    arrays = {
        "x": L0_attn_x,
        "w_qkv_t": np.asarray(L0_attn_w_qkv).T,
        "b_qkv": L0_attn_b_qkv,
        "w_out_t": np.asarray(L0_attn_w_out).T,
        "b_out": L0_attn_b_out,
        "w_router": L0_ffn_router_kernel_DE,
        "w_gate": L0_ffn_kernel_gating_EDF,
        "w_up": L0_ffn_kernel_up_EDF,
        "w_down": L0_ffn_kernel_down_EFD,
    }
    arrays = {n: np.ascontiguousarray(a) for n, a in arrays.items()}
    nc = bacc.Bacc("TRN2", target_bir_lowering=False, num_devices=1)
    args = [nc.dram_tensor(n, a.shape, mybir.dt.from_np(a.dtype), kind="ExternalInput").ap()
            for n, a in arrays.items()]
    shape = arrays["x"].shape
    args.append(nc.dram_tensor("out", shape, mybir.dt.from_np(arrays["x"].dtype), kind="ExternalOutput").ap())
    attn_moe_kernel(nc, *args)
    r = run(nc, [arrays], core_ids=[0])
    return r.results[0]["out"]
```
